# Optimizing a Trainium2 kernel written in Bass

```python
import numpy as np
import jax
import jax.numpy as jnp

def _softmax(x, axis=-1):
    return jax.nn.softmax(x, axis=axis)

def _gelu(x):
    return jax.nn.gelu(x, approximate=True)

def _silu(x):
    return jax.nn.silu(x)

def _sigmoid(x):
    return jax.nn.sigmoid(x)

def _layernorm(x, axis=-1, eps=1e-05):
    m = jnp.mean(x, axis=axis, keepdims=True)
    v = jnp.var(x, axis=axis, keepdims=True)
    return (x - m) / jnp.sqrt(v + eps)

def _scatter_add(tgt, idx, src, axis=0):
    return tgt.at[idx].add(src)

def _segment_sum(src, seg, n):
    return jax.ops.segment_sum(src, seg, n)
kernel_name = 'mk_recurrent_d1_jaxref_r4_32292f'

def setup_inputs(seed: int=0):
    np.random.seed(seed)
    _w = jnp.asarray

    def _L0_attn_setup():
        import jax, jax.numpy as jnp
        import numpy as np
        B_, L_, D_RES, D_INNER, N_STATE, K_CONV = (2, 256, 256, 128, 64, 3)

        def _causal_dwconv(x, w, b):
            xt = jnp.transpose(x, (0, 2, 1))
            k = w.shape[-1]
            out = jax.lax.conv_general_dilated(xt, w, (1,), [(k - 1, 0)], feature_group_count=w.shape[0])
            return jnp.transpose(out, (0, 2, 1)) + b

        def _s6(u, W_delta, b_delta, W_B, W_C, A_log, D):
            A = -jnp.exp(A_log)
            delta = jax.nn.softplus(u @ W_delta + b_delta)
            Bm = u @ W_B
            Cm = u @ W_C

            def step(h, inputs):
                u_t, d_t, b_t, c_t = inputs
                dA = jnp.exp(d_t[..., None] * A)
                h = dA * h + (d_t * u_t)[..., None] * b_t[:, None, :]
                y = jnp.einsum('bdn,bn->bd', h, c_t)
                return (h, y)
            h0 = jnp.zeros((u.shape[0], A.shape[0], A.shape[1]), u.dtype)
            xs = (jnp.swapaxes(u, 0, 1), jnp.swapaxes(delta, 0, 1), jnp.swapaxes(Bm, 0, 1), jnp.swapaxes(Cm, 0, 1))
            _, ys = jax.lax.scan(step, h0, xs)
            return jnp.swapaxes(ys, 0, 1) + u * D
        key = jax.random.key(seed)
        ks = jax.random.split(key, 8)
        s = lambda k, shp, sc: jax.random.normal(k, shp, dtype=jnp.float32) * sc
        return {'x': s(ks[0], (B_, L_, D_RES), 1.0), 'ln_gamma': jnp.ones((D_RES,), jnp.float32), 'ln_beta': jnp.zeros((D_RES,), jnp.float32), 'W_up': s(ks[1], (D_RES, 2 * D_INNER), 0.02), 'b_up': jnp.zeros((2 * D_INNER,), jnp.float32), 'conv_w': s(ks[2], (D_INNER, 1, K_CONV), 0.2), 'conv_b': jnp.zeros((D_INNER,), jnp.float32), 'W_delta': s(ks[3], (D_INNER, D_INNER), 0.02), 'b_delta': jnp.full((D_INNER,), -4.0, jnp.float32), 'W_B': s(ks[4], (D_INNER, N_STATE), 0.02), 'W_C': s(ks[5], (D_INNER, N_STATE), 0.02), 'A_log': jnp.log(jnp.broadcast_to(jnp.arange(1, N_STATE + 1, dtype=jnp.float32), (D_INNER, N_STATE))).copy(), 'D': jnp.ones((D_INNER,), jnp.float32), 'W_down': s(ks[6], (D_INNER, D_RES), 0.02), 'b_down': jnp.zeros((D_RES,), jnp.float32)}
    _L0_attn_in = _L0_attn_setup()

    def _L0_ffn_setup():
        import jax, jax.numpy as jnp
        import numpy as np
        W_SCALE = 0.02
        TOP_K = 2
        key = jax.random.key(seed)
        ks = jax.random.split(key, 5)
        B, S, H, I, E = (2, 256, 256, 1024, 8)
        return {'x': jax.random.normal(ks[0], (B, S, H), dtype=jnp.float32), 'gate': jax.random.normal(ks[1], (H, E), dtype=jnp.float32) * W_SCALE, 'experts_w1': jax.random.normal(ks[2], (E, H, I), dtype=jnp.float32) * W_SCALE, 'experts_w2': jax.random.normal(ks[3], (E, I, H), dtype=jnp.float32) * W_SCALE, 'experts_w3': jax.random.normal(ks[4], (E, H, I), dtype=jnp.float32) * W_SCALE}
    _L0_ffn_in = _L0_ffn_setup()
    _d = {'L0_attn_x': _L0_attn_in['x'], 'L0_attn_ln_gamma': _L0_attn_in['ln_gamma'], 'L0_attn_ln_beta': _L0_attn_in['ln_beta'], 'L0_attn_W_up': _L0_attn_in['W_up'], 'L0_attn_b_up': _L0_attn_in['b_up'], 'L0_attn_conv_w': _L0_attn_in['conv_w'], 'L0_attn_conv_b': _L0_attn_in['conv_b'], 'L0_attn_W_delta': _L0_attn_in['W_delta'], 'L0_attn_b_delta': _L0_attn_in['b_delta'], 'L0_attn_W_B': _L0_attn_in['W_B'], 'L0_attn_W_C': _L0_attn_in['W_C'], 'L0_attn_A_log': _L0_attn_in['A_log'], 'L0_attn_D': _L0_attn_in['D'], 'L0_attn_W_down': _L0_attn_in['W_down'], 'L0_attn_b_down': _L0_attn_in['b_down'], 'L0_ffn_gate': _L0_ffn_in['gate'], 'L0_ffn_experts_w1': _L0_ffn_in['experts_w1'], 'L0_ffn_experts_w2': _L0_ffn_in['experts_w2'], 'L0_ffn_experts_w3': _L0_ffn_in['experts_w3']}
    _x0 = _d['L0_attn_x']
    _d['L0_attn_x'] = jax.random.normal(jax.random.fold_in(jax.random.key(seed), 1), (1, 4096, 256), dtype=_x0.dtype)
    del _x0
    return _d

def reference(L0_attn_x, L0_attn_ln_gamma, L0_attn_ln_beta, L0_attn_W_up, L0_attn_b_up, L0_attn_conv_w, L0_attn_conv_b, L0_attn_W_delta, L0_attn_b_delta, L0_attn_W_B, L0_attn_W_C, L0_attn_A_log, L0_attn_D, L0_attn_W_down, L0_attn_b_down, L0_ffn_gate, L0_ffn_experts_w1, L0_ffn_experts_w2, L0_ffn_experts_w3):

    def _L0_attn_ref(x, ln_gamma, ln_beta, W_up, b_up, conv_w, conv_b, W_delta, b_delta, W_B, W_C, A_log, D, W_down, b_down):
        import jax, jax.numpy as jnp
        import numpy as np
        B_, L_, D_RES, D_INNER, N_STATE, K_CONV = (2, 256, 256, 128, 64, 3)

        def _causal_dwconv(x, w, b):
            xt = jnp.transpose(x, (0, 2, 1))
            k = w.shape[-1]
            out = jax.lax.conv_general_dilated(xt, w, (1,), [(k - 1, 0)], feature_group_count=w.shape[0])
            return jnp.transpose(out, (0, 2, 1)) + b

        def _s6(u, W_delta, b_delta, W_B, W_C, A_log, D):
            A = -jnp.exp(A_log)
            delta = jax.nn.softplus(u @ W_delta + b_delta)
            Bm = u @ W_B
            Cm = u @ W_C

            def step(h, inputs):
                u_t, d_t, b_t, c_t = inputs
                dA = jnp.exp(d_t[..., None] * A)
                h = dA * h + (d_t * u_t)[..., None] * b_t[:, None, :]
                y = jnp.einsum('bdn,bn->bd', h, c_t)
                return (h, y)
            h0 = jnp.zeros((u.shape[0], A.shape[0], A.shape[1]), u.dtype)
            xs = (jnp.swapaxes(u, 0, 1), jnp.swapaxes(delta, 0, 1), jnp.swapaxes(Bm, 0, 1), jnp.swapaxes(Cm, 0, 1))
            _, ys = jax.lax.scan(step, h0, xs)
            return jnp.swapaxes(ys, 0, 1) + u * D
        mu = jnp.mean(x, -1, keepdims=True)
        var = jnp.mean((x - mu) ** 2, -1, keepdims=True)
        y = (x - mu) * jax.lax.rsqrt(var + 1e-05) * ln_gamma + ln_beta
        up = y @ W_up + b_up
        left, right = jnp.split(up, 2, axis=-1)
        left = jax.nn.silu(_causal_dwconv(left, conv_w, conv_b))
        left = _s6(left, W_delta, b_delta, W_B, W_C, A_log, D)
        gated = left * jax.nn.silu(right)
        return x + gated @ W_down + b_down

    def _L0_ffn_ref(x, gate, experts_w1, experts_w2, experts_w3):
        import jax, jax.numpy as jnp
        import numpy as np
        W_SCALE = 0.02
        TOP_K = 2
        E = experts_w1.shape[0]
        router_logits = jnp.einsum('bsh,he->bse', x, gate)
        routing_weights, selected = jax.lax.top_k(router_logits, TOP_K)
        routing_weights = jax.nn.softmax(routing_weights, axis=-1)
        onehot = jax.nn.one_hot(selected, E, dtype=x.dtype)
        tok_w = jnp.einsum('bsk,bske->bse', routing_weights, onehot)
        g = jnp.einsum('bsh,ehi->ebsi', x, experts_w1)
        u = jnp.einsum('bsh,ehi->ebsi', x, experts_w3)
        hid = jax.nn.silu(g) * u
        eo = jnp.einsum('ebsi,eih->ebsh', hid, experts_w2)
        out = jnp.einsum('ebsh,bse->bsh', eo, tok_w)
        return out
    x = L0_attn_x
    xn = _layernorm(x, axis=-1)
    s = _L0_attn_ref(xn, L0_attn_ln_gamma, L0_attn_ln_beta, L0_attn_W_up, L0_attn_b_up, L0_attn_conv_w, L0_attn_conv_b, L0_attn_W_delta, L0_attn_b_delta, L0_attn_W_B, L0_attn_W_C, L0_attn_A_log, L0_attn_D, L0_attn_W_down, L0_attn_b_down)
    g = _silu(_L0_ffn_ref(xn, L0_ffn_gate, L0_ffn_experts_w1, L0_ffn_experts_w2, L0_ffn_experts_w3))
    x = x + s * g
    return x

_drawn_inputs = setup_inputs


def setup_inputs(seed=0):
    import zlib

    import numpy as np

    out = dict(_drawn_inputs(seed))
    spreads = {'L0_attn_ln_gamma': (1.0, 0.2),
     'L0_attn_ln_beta': (0.0, 0.1),
     'L0_attn_b_up': (0.0, 0.1),
     'L0_attn_conv_b': (0.0, 0.1),
     'L0_attn_b_delta': (-4.0, 0.2),
     'L0_attn_D': (1.0, 0.2),
     'L0_attn_b_down': (0.0, 0.1)}
    factors = {}
    for name, (base, spread) in spreads.items():
        noise = np.random.default_rng([zlib.crc32(name.encode()), seed]).standard_normal(out[name].shape)
        drawn = base * np.exp(spread * noise) if base else spread * noise
        out[name] = jnp.asarray(drawn.astype(out[name].dtype))
    for name, factor in factors.items():
        out[name] = (out[name] * factor).astype(out[name].dtype)
    return out
```

```python
from contextlib import ExitStack

import numpy as np
import concourse.bass as bass
from concourse import mybir

P = 128
T, D, E, I, N = 4096, 256, 8, 1024, 64
NT = T // P
CH = 512
NC = T // CH
TC = CH // P
PAIRS = P // 2
QUADS = PAIRS // 4
SLOT = 256
TILES = 2 * T // SLOT + E
KS = I // P
WROW = 2 * 2 * P + D
BODY = 2
BODIES = NC // BODY
ITS = BODY * PAIRS
BT = TILES // BODIES
USES = 1 + KS
W_RING, H_RING, P_RING, A_RING = 5, 8, 8, 4
EPS = 1e-5

F32, F32R, I32, U32 = mybir.dt.float32, mybir.dt.float32r, mybir.dt.int32, mybir.dt.uint32
ALU, ACT, AX = mybir.AluOpType, mybir.ActivationFunctionType, mybir.AxisListType
ds = bass.ds

assert TILES % BODIES == 0 and (BT * KS) % W_RING == 0 and (BT * USES) % 2 == 0 and BT % 2 == 0


def body_order():
    turns = [(t, r) for t in range(BT) for r in range(USES)]
    order, done = [], 0
    for s in range(ITS):
        order.append(("scan", s, 0))
        while done < (s + 1) * len(turns) // ITS:
            order.append(("turn", *turns[done]))
            done += 1
    return order


def mamba_and_experts(nc, x, gam, bet, w_up, b_up, conv_w, conv_b, w_dl, b_dl, w_b2, w_c2, a_log,
                      dvec, w_dn, b_dn, gate, w13, w2, c_ident, c_upper, c_pick, c_win, c_first,
                      c_start, out):
    with ExitStack() as ctx:
        def sb(name, shape, dt=F32):
            return ctx.enter_context(nc.sbuf_tensor(name, shape, dt))

        def sem(name):
            return ctx.enter_context(nc.semaphore(name))

        x_sorted = nc.dram_tensor("x_sorted", [TILES * SLOT, D], F32).ap()
        y_sorted = nc.dram_tensor("y_sorted", [TILES * SLOT, D], F32).ap()
        parts_d = nc.dram_tensor("parts_d", [2, 2, P, T], F32).ap()
        tails_d = nc.dram_tensor("tails_d", [P, 2, T], F32).ap()

        xn = sb("xn", [P, NT, D])
        u = sb("u", [P, T])
        b_rep = sb("b_rep", [P, T])
        c_rep = sb("c_rep", [P, T + 2])
        wring = sb("wring", [P, W_RING, WROW])
        arena = sb("arena", [P, (H_RING + P_RING + 2 * A_RING) * CH])
        stack = sb("stack", [P, 2, 2, 2, CH], F32R)
        pick = sb("pick", [P, 32, P], F32R)
        tails = sb("tails", [P, 2, CH])
        carry = sb("carry", [P, PAIRS])
        a_neg = sb("a_neg", [P, PAIRS])
        xg = sb("xg", [P, 1, 2, D])
        c_now = sb("c_now", [P, BODY, CH])
        xgT = sb("xgT", [P, 2, 2, SLOT])
        o_sb = sb("o_sb", [P, 2, 2, D])
        th = sb("th", [P, 2, SLOT])
        gt = sb("gt", [P, 2, SLOT])
        hid = sb("hid", [P, 4, SLOT])
        ident = sb("ident", [P, P])
        ones = sb("ones", [P, P])
        win = sb("win", [P, 62])
        first = sb("first", [P, E])
        start = sb("start", [P, TILES])
        wup = hid[:, 0:2, :]
        upper, cpick = hid[:, 2, 0:P], hid[:, 2, P:P + 64]
        wdl = sb("wdl", [P, P])
        wbc = sb("wbc", [P, 2, P])
        wdn = sb("wdn", [P, D])
        gsb = sb("gsb", [P, 2, E])
        vec = sb("vec", [P, 16])
        half = sb("half", [P, 8])
        bdn = sb("bdn", [P, D])
        prob = sb("prob", [P, 2, NT])
        slot_i = sb("slot_i", [P, 2, NT], U32)
        row_i = sb("row_i", [P, TILES], I32)

        ring = arena[:, :].rearrange("p (r t) -> p r t", t=CH)
        h_ring, p_ring = ring[:, 0:H_RING, :], ring[:, H_RING:H_RING + P_RING, :]
        a_ring = ring[:, H_RING + P_RING:H_RING + P_RING + A_RING, :]
        b_ring = ring[:, H_RING + P_RING + A_RING:H_RING + P_RING + 2 * A_RING, :]
        yh = arena[:, 0:NT * D].rearrange("p (n c) -> p n c", c=D)
        yT = ring[:, 16:18, :]
        xT = ring[:, 18:20, :]
        cv, thl, thr, sr = ring[:, 0, :], ring[:, 1, :], ring[:, 2, :], ring[:, 3, :]
        ab, ex, lg1 = ring[:, 4, :], ring[:, 5, :], ring[:, 6, :]
        wm, mx, dlt, du = ring[:, 7, :], ring[:, 8, :], ring[:, 9, :], ring[:, 10, :]
        hilo = ring[:, 11:15, :]
        udr = ring[:, 15, :]
        zeros = stack[:, 1, :, :, :].rearrange("p q h t -> p (q h t)").bitcast(F32)

        stat = ring[:, 20, 0:6 * NT].rearrange("p (n k) -> p n k", k=6)
        mv = ring[:, 20, 192:192 + 2 * NT].rearrange("p (n k) -> p n k", k=2)
        rs, ve, root = (ring[:, 20, 256 + NT * k:256 + NT * (k + 1)] for k in range(3))

        def small(k, n=NT * E):
            return ring[:, 16 + k // 2, (k % 2) * 256:(k % 2) * 256 + n]

        banks = [ctx.enter_context(nc.psum_tensor(f"bank{i}", [P, 512], F32)) for i in range(8)]
        dl_bank, du_bank, y_bank = banks[0:2], banks[2:4], banks[4]
        gu_bank, o_bank = banks[5:7], banks[7]

        s_x, s_cst, s_zero, s_ones, s_zd = (sem(k) for k in ("s_x", "s_cst", "s_zero", "s_ones", "s_zd"))
        s_setup, s_aneg, s_norm, s_stat, s_root = (sem(k) for k in ("s_setup", "s_aneg", "s_norm", "s_stat", "s_root"))
        s_tr, s_trev, s_lr, s_lrev, s_logit = (sem(k) for k in ("s_tr", "s_trev", "s_lr", "s_lrev", "s_logit"))
        s_rt, s_rex, s_rex2, s_cnt, s_slot, s_scat = (sem(k) for k in ("s_rt", "s_rex", "s_rex2", "s_cnt", "s_slot", "s_scat"))
        s_cv, s_thr, s_thl, s_u, s_dv = (sem(k) for k in ("s_cv", "s_thr", "s_thl", "s_u", "s_dv"))
        s_dp, s_bc, s_bcev, s_sp = (sem(k) for k in ("s_dp", "s_bc", "s_bcev", "s_sp"))
        s_dlt, s_partd = sem("s_dlt"), sem("s_partd")
        s_stack = [sem("s_stack0"), sem("s_stack1")]
        s_tails, s_sel, s_exp, s_bm, s_scan = (sem(k) for k in ("s_tails", "s_sel", "s_exp", "s_bm", "s_scan"))
        s_carry, s_hc, s_red, s_gated, s_yr = (sem(k) for k in ("s_carry", "s_hc", "s_red", "s_gated", "s_yr"))
        s_xg = [sem("s_xg0"), sem("s_xg1")]
        s_w = [sem(f"s_w{i}") for i in range(W_RING)]
        s_gu, s_xgT, s_th, s_gt, s_hid = (sem(k) for k in ("s_gu", "s_xgT", "s_th", "s_gt", "s_hid"))
        s_o, s_oev = sem("s_o"), sem("s_oev")
        s_store = [sem("s_store0"), sem("s_store1")]
        s_dn, s_s, s_fin, s_ga, s_xr, s_out = (sem(k) for k in ("s_dn", "s_s", "s_fin", "s_ga", "s_xr", "s_out"))
        s_gs, s_tf, s_f, s_mix, s_cnow = (sem(k) for k in ("s_gs", "s_tf", "s_f", "s_mix", "s_cnow"))

        ORDER = body_order()
        TURNS = BT * USES

        def ge(eng, s, b, per_body, n):
            if isinstance(b, int) and b * per_body + n <= 0:
                return
            eng.wait_ge(s, b * per_body + n)

        def after(eng, s, value):
            if not isinstance(value, int) or value > 0:
                eng.wait_ge(s, value)

        def chunks(eng, step):
            step(0)
            with eng.Fori(1, NC) as c:
                step(c)

        def bodies(eng, body):
            body(0)
            with eng.Fori(1, BODIES) as b:
                body(b)

        KD = 9
        block = ctx.enter_context(nc.Block())

        @block.sync
        def _(sp):
            sp.dma_start(xn[:, :, :], x.rearrange("a (n p) c -> p (a n) c", p=P)).then_inc(s_x, 16)
            for dst, src in ((ident[:, :], c_ident), (upper, c_upper), (win[:, :], c_win),
                             (first[:, :], c_first), (start[:, :], c_start), (cpick, c_pick),
                             (wup, w_up.rearrange("(h p) c -> p h c", p=P)), (wdl[:, :], w_dl),
                             (wbc[:, 0, :], w_b2), (wbc[:, 1, :], w_c2), (wdn[:, :], w_dn),
                             (gsb[:, :, :], gate.rearrange("(h p) e -> p h e", p=P)), (a_neg[:, :], a_log),
                             (vec[:, 0:2], gam), (vec[:, 2:4], bet), (vec[:, 4:6], b_up),
                             (vec[:, 6:9], conv_w), (vec[:, 9:10], conv_b), (vec[:, 10:11], b_dl),
                             (vec[:, 11:12], dvec), (bdn[:, :], b_dn.partition_broadcast(P))):
                sp.dma_start(dst, src).then_inc(s_cst, 16)
            sp.wait_ge(s_zero, 1)
            zrows = x_sorted.rearrange("(q p r) c -> q p (r c)", p=P, r=8)
            for q in range(TILES * SLOT // (8 * P)):
                sp.dma_start(zrows[q], zeros).then_inc(s_zd, 16)
            def store_parts(c):
                t0 = c * CH
                sp.wait_ge(s_dlt, (c + 1) * KD)
                for q in range(2):
                    for k in range(2):
                        for h in range(2):
                            sp.dma_start(parts_d[q, h, 64 * k:64 * k + 64, ds(t0, CH)],
                                         hilo[64 * h:64 * h + 64, 2 * q + k, :]).then_inc(s_partd, 16)
                sp.dma_start(tails_d[:, 0, ds(t0, CH)], sr).then_inc(s_partd, 16)
                sp.dma_start(tails_d[:, 1, ds(t0, CH)], udr).then_inc(s_partd, 16)

            chunks(sp, store_parts)
            sp.wait_ge(s_partd, 160 * NC)
            sp.wait_ge(s_slot, 1)

            def load_stack(b, k):
                for q in range(2):
                    sp.dma_start(stack[:, k, q, :, :].bitcast(F32),
                                 parts_d[q, :, :, ds((b * BODY + k) * CH, CH)].rearrange("h p t -> p h t")
                                 ).then_inc(s_stack[k], 16)

            sp.wait_ge(s_zd, 16 * (TILES * SLOT // (8 * P)))
            sp.wait_ge(s_scat, 16 * 2 * NT)

            def body(b):
                state = {}
                ge(sp, s_sel, b, ITS, -PAIRS)
                load_stack(b, 0)
                for kind, i, r in ORDER:
                    if kind == "scan" and i == 8:
                        ge(sp, s_sel, b, ITS, 0)
                        load_stack(b, 1)
                    if kind == "scan" and i % PAIRS == 16:
                        k = i // PAIRS
                        ge(sp, s_gated, b, BODY, k)
                        sp.dma_start(tails[:, :, :], tails_d[:, :, ds((b * BODY + k) * CH, CH)]).then_inc(s_tails, 16)
                    if kind == "turn":
                        n = USES * i + r
                        if r == 0:
                            ge(sp, s_gu, b, TURNS, USES * (i - 1) + 1)
                            sp.dma_start(xg[:, 0, :, :],
                                         x_sorted[ds(b * (BT * SLOT) + i * SLOT, SLOT), :].rearrange("(s p) c -> p s c", p=P)
                                         ).then_inc(s_xg[i % 2], 16)
                            state["row"] = sp.value_load(row_i[0:1, ds(b * BT + i, 1)], min_val=0, max_val=(E - 1) * KS)
                        else:
                            k = KS * i + r - 1
                            ge(sp, s_o, b, BT * KS, k - W_RING + 1)
                            at = state["row"] + (r - 1)
                            sp.dma_start(wring[:, k % W_RING, 0:4 * P],
                                         w13[ds(at, 1), :, :].rearrange("a p c -> p (a c)")).then_inc(s_w[k % W_RING], 16)
                            sp.dma_start(wring[:, k % W_RING, 4 * P:WROW],
                                         w2[ds(at, 1), :, :].rearrange("a p c -> p (a c)")).then_inc(s_w[k % W_RING], 16)

            bodies(sp, body)
            sp.wait_ge(s_gated, NC)
            def load_residual_store_out(c):
                sp.dma_start(ring[:, 16:18, :].rearrange("p a t -> p (a t)").rearrange("p (n c) -> p n c", c=D),
                             x[0, ds(c * CH, CH), :].rearrange("(n p) c -> p n c", p=P)).then_inc(s_xr, 16)
                sp.wait_ge(s_fin, c + 1)
                sp.dma_start(out[0, ds(c * CH, CH), :].rearrange("(n p) c -> p n c", p=P),
                             ring[:, 18:20, :].rearrange("p a t -> p (a t)").rearrange("p (n c) -> p n c", c=D)
                             ).then_inc(s_out, 16)

            chunks(sp, load_residual_store_out)
            sp.wait_ge(s_out, 16 * NC)

        @block.gpsimd
        def _(pool):
            pool.wait_ge(s_slot, 1)
            pool.wait_ge(s_zd, 16 * (TILES * SLOT // (8 * P)))
            for k in range(2):
                for n in range(NT):
                    pool.indirect_dma_start(x_sorted, bass.IndirectOffsetOnAxis(slot_i[:, k, n:n + 1], 0),
                                            xn[:, n, :], None).then_inc(s_scat, 16)

            def body(b):
                for kind, s, _ in ORDER:
                    if kind == "scan":
                        k = s // PAIRS
                        if s % PAIRS == 0:
                            pool.tensor_copy(c_now[:, k, :], c_rep[:, ds((b * BODY + k) * CH + 2, CH)]).then_inc(s_cnow, 1)
                            ge(pool, s_cnow, b, BODY, k + 1)
                        ge(pool, s_scan, b, ITS, s + 1)
                        ge(pool, s_red, b, ITS // 4, (s - P_RING) // 4 + 1)
                        pool.tensor_tensor(p_ring[:, s % P_RING, :], h_ring[:, s % H_RING, :], c_now[:, k, :],
                                           ALU.mult).then_inc(s_hc, 1)

            pool.wait_ge(s_bcev, 2 * NC)
            pool.wait_ge(s_scat, 16 * 2 * NT)
            bodies(pool, body)
            pool.wait_ge(s_carry, NC * QUADS)
            for k in range(2):
                pool.wait_ge(s_store[k], 16 * TILES // 2)
            for c in range(NC):
                if c >= 2:
                    pool.wait_ge(s_f, TC * (c - 1))
                for k in range(2):
                    for n in range(TC):
                        pool.indirect_dma_start(ring[:, 2 * (2 * (c % 2) + k):2 * (2 * (c % 2) + k) + 2, :].rearrange("p a t -> p (a t)")[:, n * D:(n + 1) * D],
                                                None, y_sorted,
                                                bass.IndirectOffsetOnAxis(slot_i[:, k, TC * c + n:TC * c + n + 1], 0)
                                                ).then_inc(s_ga, 16)
                pool.wait_ge(s_ga, 16 * 2 * TC * (c + 1))

        @block.scalar
        def _(act):
            act.wait_ge(s_cst, 16 * 21)
            act.activation(a_neg[:, :], a_neg[:, :], ACT.Exp).then_inc(s_aneg, 1)
            for k in range(2):
                act.wait_ge(s_stat, 3 + 9 * k)
                act.activation(root, ve, ACT.Sqrt).then_inc(s_root, 1)
            act.wait_ge(s_setup, 1)
            def evict_projections(c):
                act.wait_ge(s_tr, c + 1)
                after(act, s_logit, c)
                for h in range(2):
                    act.activation(yT[:, h, :], banks[h][:, :], ACT.Identity, bias=vec[:, 2 + h:3 + h],
                                   scale=vec[:, h:h + 1])
                for h in range(2):
                    ins = act.activation(xT[:, h, :], banks[2 + h][:, :], ACT.Copy)
                ins.then_inc(s_trev, 1)
                act.wait_ge(s_lr, c + 1)
                act.activation(c_rep[:, ds(c * CH + 2, CH)], banks[4][:, :], ACT.Identity, bias=vec[:, 4:5])
                act.activation(b_rep[:, ds(c * CH, CH)], banks[5][:, :], ACT.Identity, bias=half[:, 4:5],
                               scale=0.5).then_inc(s_lrev, 1)

            chunks(act, evict_projections)
            act.wait_ge(s_rex, 1)
            act.activation(small(4, NT), small(3, NT), ACT.Exp).then_inc(s_rex2, 1)
            def silu_and_softplus(c):
                after(act, s_dv, c)
                act.activation(thr, b_rep[:, ds(c * CH, CH)], ACT.Tanh).then_inc(s_thr, 1)
                act.wait_ge(s_cv, c + 1)
                act.activation(thl, cv, ACT.Tanh).then_inc(s_thl, 1)
                act.wait_ge(s_dp, c + 1)
                act.activation(ab, banks[0][:, :], ACT.Abs, bias=vec[:, 10:11]).then_inc(s_sp, 1)
                act.wait_ge(s_sp, 3 * c + 1)
                act.activation(ex, ab, ACT.Exp, scale=-1.0).then_inc(s_sp, 1)
                act.wait_ge(s_sp, 3 * c + 2)
                act.activation(lg1, ex, ACT.Ln, bias=1.0).then_inc(s_sp, 1)

            chunks(act, silu_and_softplus)
            act.wait_ge(s_u, NC)
            act.wait_ge(s_dv, NC)
            def evict_b_and_c(c):
                act.wait_ge(s_bc, c + 1)
                act.activation(b_rep[:, ds(c * CH, CH)], banks[1][:, :], ACT.Copy).then_inc(s_bcev, 1)
                act.activation(c_rep[:, ds(c * CH + 2, CH)], banks[2][:, :], ACT.Copy).then_inc(s_bcev, 1)

            chunks(act, evict_b_and_c)
            act.wait_ge(s_partd, 160 * NC)

            def evict_out(b, i):
                ge(act, s_o, b, BT * KS, KS * (i + 1))
                ge(act, s_store[i % 2], b, 16 * BT // 2, 16 * ((i - 2) // 2 + 1))
                act.activation(o_sb[:, i % 2, :, :].rearrange("p s c -> p (s c)"), o_bank[:, :], ACT.Copy).then_inc(s_oev, 1)
                ge(act, s_oev, b, BT, i + 1)
                act.dma_start(y_sorted[ds(b * (BT * SLOT) + i * SLOT, SLOT), :].rearrange("(s p) c -> p s c", p=P),
                              o_sb[:, i % 2, :, :]).then_inc(s_store[i % 2], 16)

            def save_carry(b, q):
                ge(act, s_scan, b, ITS, 4 * q + 4)
                r, k = (4 * q) % H_RING, q % QUADS
                act.activation(carry[:, 4 * k:4 * k + 4], h_ring[:, r:r + 4, CH - 1], ACT.Copy).then_inc(s_carry, 1)

            def body(b):
                for kind, i, r in ORDER:
                    if kind == "scan":
                        s = i
                        q = s % PAIRS
                        ge(act, s_sel, b, ITS, s + 1)
                        ge(act, s_scan, b, ITS, s - A_RING + 1)
                        act.activation(a_ring[:, s % A_RING, :], dl_bank[s % 2][:, :], ACT.Exp,
                                       scale=a_neg[:, q:q + 1]).then_inc(s_exp, 1)
                        if s % 4 == 1 and s >= 5:
                            save_carry(b, (s - 5) // 4)
                    elif r == 0:
                        ge(act, s_gu, b, TURNS, USES * i + 1)
                        ge(act, s_gu, b, TURNS, USES * (i - 2) + USES)
                        act.activation(xgT[:, i % 2, :, :].rearrange("p h s -> p (h s)"),
                                       gu_bank[(USES * i) % 2][:, :], ACT.Copy).then_inc(s_xgT, 1)
                    else:
                        k = KS * i + r - 1
                        ge(act, s_gu, b, TURNS, USES * i + r + 1)
                        ge(act, s_hid, b, BT * KS, k - 1)
                        act.activation(th[:, k % 2, :], gu_bank[(USES * i + r) % 2][:, 0:SLOT], ACT.Tanh,
                                       scale=0.5).then_inc(s_th, 1)
                        if r == 1 and i > 0:
                            evict_out(b, i - 1)
                save_carry(b, ITS // 4 - 1)
                evict_out(b, BT - 1)

            bodies(act, body)
            for c in range(NC):
                for n in range(TC):
                    act.wait_ge(s_ga, 16 * 2 * TC * (c + 1))
                    g0 = ring[:, 4 * (c % 2):4 * (c % 2) + 2, :].rearrange("p a t -> p (a t)")[:, n * D:(n + 1) * D]
                    act.activation(g0, g0, ACT.Identity, scale=prob[:, 0, TC * c + n:TC * c + n + 1]).then_inc(s_gs, 1)
                act.wait_ge(s_f, TC * (c + 1))
                act.activation(ring[:, 12:14, :], ring[:, 10:12, :], ACT.Tanh, scale=0.5).then_inc(s_tf, 1)

        @block.vector
        def _(v):
            v.memset(zeros, 0.0).then_inc(s_zero, 1)
            v.memset(ones[:, :], 1.0).then_inc(s_ones, 1)
            v.memset(carry[:, :], 0.0)
            v.memset(c_rep[:, 0:2], 0.0)
            v.wait_ge(s_cst, 16 * 21)
            v.tensor_copy(pick[:, :, :].rearrange("p a (b k) -> p (a b) k", b=2),
                          cpick.unsqueeze(2).broadcast_to([P, 64, 64]))
            v.tensor_scalar(half[:, 0:3], vec[:, 6:9], 0.5, None, ALU.mult)
            v.tensor_scalar(half[:, 3:4], vec[:, 9:10], 0.5, None, ALU.mult)
            v.tensor_scalar(half[:, 4:5], vec[:, 5:6], 0.5, None, ALU.mult).then_inc(s_setup, 1)
            v.wait_ge(s_aneg, 1)
            v.tensor_scalar(a_neg[:, :], a_neg[:, :], -1.0, None, ALU.mult).then_inc(s_setup, 1)

            v.wait_ge(s_x, 16)
            n_st = [0]

            def stat_step(ins):
                n_st[0] += 1
                ins.then_inc(s_stat, 1)
                v.wait_ge(s_stat, n_st[0])

            def inverse_deviation(k):
                stat_step(v.tensor_scalar(ve, mv[:, :, 1], EPS, None, ALU.add))
                v.wait_ge(s_root, k + 1)
                stat_step(v.reciprocal(rs, root))
                stat_step(v.tensor_tensor(root, rs, rs, ALU.mult))
                stat_step(v.tensor_tensor(root, root, ve, ALU.mult))
                stat_step(v.tensor_scalar(root, root, -0.5, 1.5, ALU.mult, ALU.add))
                stat_step(v.tensor_tensor(rs, rs, root, ALU.mult))

            def moments(src):
                for n in range(NT):
                    ins = v.bn_stats(stat[:, n, :], src[:, n, :])
                stat_step(ins)
                for n in range(NT):
                    ins = v.bn_aggr(mv[:, n, :], stat[:, n, :])
                stat_step(ins)

            moments(xn)
            inverse_deviation(0)
            for n in range(NT):
                ins = v.tensor_scalar(xn[:, n, :], xn[:, n, :], mv[:, n, 0:1], rs[:, n:n + 1], ALU.subtract, ALU.mult)
            stat_step(ins)
            moments(xn)
            inverse_deviation(1)
            for n in range(NT):
                ins = v.tensor_scalar(yh[:, n, :], xn[:, n, :], mv[:, n, 0:1], rs[:, n:n + 1], ALU.subtract, ALU.mult)
                if n % TC == TC - 1:
                    ins.then_inc(s_norm, 1)
            v.wait_ge(s_norm, NC)

            n_rt = [0]

            def link(ins):
                n_rt[0] += 1
                ins.then_inc(s_rt, 1)
                v.wait_ge(s_rt, n_rt[0])

            v.wait_ge(s_logit, NC)
            v.wait_ge(s_trev, NC)

            def ne(a):
                return a.rearrange("p (n e) -> p n e", e=E)

            def wide(a):
                return a.unsqueeze(2).broadcast_to([P, NT, E])

            lg, cand, hot1, hot2, msk = small(0), small(1), small(5), small(6), small(7)
            m1, m2, dd, pe_, den = small(2, NT), ring[:, 17, 32:64], small(3, NT), small(4, NT), ring[:, 17, 64:96]
            descend = first[:, :].unsqueeze(1).broadcast_to([P, NT, E])
            link(v.tensor_copy(lg, banks[6][:, 0:NT * E]))

            def one_hot(top, hot):
                link(v.tensor_reduce(top, ne(lg), AX.X, ALU.max))
                link(v.tensor_tensor(ne(cand), ne(lg), wide(top), ALU.is_equal))
                link(v.tensor_tensor(ne(cand), ne(cand), descend, ALU.mult))
                link(v.tensor_reduce(den, ne(cand), AX.X, ALU.max))
                link(v.tensor_tensor(ne(hot), ne(cand), wide(den), ALU.is_equal))

            one_hot(m1, hot1)
            link(v.scalar_tensor_tensor(out=lg, in0=hot1, scalar=-3.0e38, in1=lg, op0=ALU.mult, op1=ALU.add))
            one_hot(m2, hot2)
            v.tensor_tensor(dd, m2, m1, ALU.subtract).then_inc(s_rex, 1)
            v.tensor_tensor(msk.rearrange("p (e n) -> p n e", n=NT), ne(hot1), ne(hot2), ALU.add).then_inc(s_cnt, 1)
            v.wait_ge(s_rex2, 1)
            link(v.tensor_scalar(den, pe_, 1.0, None, ALU.add))
            link(v.reciprocal(den, den))
            link(v.tensor_scalar(prob[:, 0, :], den, 0.5, None, ALU.mult))
            link(v.tensor_tensor(prob[:, 1, :], prob[:, 0, :], pe_, ALU.mult))
            incl, excl, slotf, tmp = small(8), small(9), small(10), small(1)
            ev = incl.rearrange("p (e n) -> p e n", n=NT)
            xv = excl.rearrange("p (e n) -> p e n", n=NT)
            cnt, pad, ends, shift, rem = (ring[:, 17, 96 + 8 * k:104 + 8 * k] for k in range(5))
            v.wait_ge(s_cnt, 2)
            v.wait_ge(s_ones, 1)
            link(v.memset(small(11), 1.0))
            link(v.tensor_tensor_scan(out=incl, data0=small(11),
                                      data1=banks[7][:, 256:512], initial=0.0, op0=ALU.mult, op1=ALU.add))
            link(v.tensor_tensor(excl, incl, banks[7][:, 256:512], ALU.subtract))
            link(v.tensor_tensor(cnt, ev[:, :, NT - 1], xv[:, :, 0], ALU.subtract))
            te = ring[:, 16, 0:E * TILES].rearrange("p (e t) -> p e t", t=TILES)
            link(v.tensor_tensor(te, start[:, :].unsqueeze(1).broadcast_to([P, E, TILES]),
                                 cnt.unsqueeze(2).broadcast_to([P, E, TILES]), ALU.is_lt))
            link(v.tensor_reduce(rem, te, AX.X, ALU.add))
            link(v.tensor_scalar(pad, rem, float(SLOT), None, ALU.mult))
            link(v.tensor_tensor_scan(out=ends, data0=ones[:, 0:E], data1=pad, initial=0.0, op0=ALU.mult, op1=ALU.add))
            link(v.tensor_tensor(shift, ends, pad, ALU.subtract))
            link(v.tensor_tensor(shift, shift, xv[:, :, 0], ALU.subtract))
            link(v.tensor_tensor(slotf, excl, banks[7][:, 0:256], ALU.add))
            link(v.tensor_tensor(slotf.rearrange("p (e n) -> p e n", n=NT), slotf.rearrange("p (e n) -> p e n", n=NT),
                                 shift.unsqueeze(2).broadcast_to([P, E, NT]), ALU.add))
            for k, hot in enumerate((hot1, hot2)):
                link(v.tensor_tensor(ne(tmp), ne(hot), slotf.rearrange("p (e n) -> p n e", n=NT), ALU.mult))
                link(v.tensor_reduce(den, ne(tmp), AX.X, ALU.add))
                link(v.tensor_copy(slot_i[:, k, :], den))
            tl = ring[:, 16, 0:TILES * E].rearrange("p (t e) -> p t e", e=E)
            link(v.tensor_tensor(tl, start[:, :].unsqueeze(2).broadcast_to([P, TILES, E]),
                                 ends.unsqueeze(1).broadcast_to([P, TILES, E]), ALU.is_ge))
            link(v.tensor_reduce(ring[:, 16, 400:400 + TILES], tl, AX.X, ALU.add))
            v.tensor_scalar(row_i[:, :], ring[:, 16, 400:400 + TILES], float(E - 1), float(KS), ALU.min, ALU.mult).then_inc(s_slot, 1)

            v.wait_ge(s_lrev, NC)
            def delta_stage(c):
                t0 = c * CH

                def step(ins, k):
                    ins.then_inc(s_dlt, 1)
                    v.wait_ge(s_dlt, c * KD + k)

                after(v, s_partd, c * 160)
                step(v.tensor_scalar(cv, c_rep[:, ds(t0 + 2, CH)], half[:, 2:3], half[:, 3:4], ALU.mult, ALU.add), 1)
                step(v.scalar_tensor_tensor(out=cv, in0=c_rep[:, ds(t0 + 1, CH)], scalar=half[:, 1:2], in1=cv,
                                            op0=ALU.mult, op1=ALU.add), 2)
                v.scalar_tensor_tensor(out=cv, in0=c_rep[:, ds(t0, CH)], scalar=half[:, 0:1], in1=cv,
                                       op0=ALU.mult, op1=ALU.add).then_inc(s_cv, 1)
                v.wait_ge(s_cv, c + 1)
                v.wait_ge(s_thr, c + 1)
                v.scalar_tensor_tensor(out=sr, in0=thr, scalar=1.0, in1=b_rep[:, ds(t0, CH)], op0=ALU.add, op1=ALU.mult)
                v.wait_ge(s_thl, c + 1)
                v.scalar_tensor_tensor(out=u[:, ds(t0, CH)], in0=thl, scalar=1.0, in1=cv, op0=ALU.add, op1=ALU.mult
                                       ).then_inc(s_u, 1)
                v.wait_ge(s_u, c + 1)
                v.scalar_tensor_tensor(out=udr, in0=u[:, ds(t0, CH)], scalar=vec[:, 11:12], in1=sr, op0=ALU.mult,
                                       op1=ALU.mult).then_inc(s_dv, 1)
                v.wait_ge(s_dp, c + 1)
                v.wait_ge(s_sp, 3 * c + 1)
                v.tensor_scalar(mx, banks[0][:, :], vec[:, 10:11], 0.0, ALU.add, ALU.max)
                v.wait_ge(s_sp, 3 * c + 2)
                step(v.tensor_scalar(wm, ex, 1.0, -1.0, ALU.add, ALU.add), 3)
                step(v.tensor_tensor(wm, wm, ex, ALU.subtract), 4)
                v.wait_ge(s_sp, 3 * c + 3)
                step(v.tensor_tensor(dlt, lg1, wm, ALU.subtract), 5)
                step(v.tensor_tensor(dlt, dlt, mx, ALU.add), 6)
                step(v.tensor_tensor(du, dlt, u[:, ds(t0, CH)], ALU.mult), 7)
                v.tensor_copy(hilo[:, 0, :].bitcast(F32R), dlt)
                step(v.tensor_copy(hilo[:, 2, :].bitcast(F32R), du), 8)
                v.tensor_tensor(hilo[:, 1, :].bitcast(F32R), dlt, hilo[:, 0, :], ALU.subtract)
                step(v.tensor_tensor(hilo[:, 3, :].bitcast(F32R), du, hilo[:, 2, :], ALU.subtract), 9)

            chunks(v, delta_stage)
            v.wait_ge(s_bcev, 2 * NC)
            v.wait_ge(s_partd, 160 * NC)

            def scan(b, s):
                q = s % PAIRS
                ge(v, s_exp, b, ITS, s + 1)
                ge(v, s_bm, b, ITS, s + 1)
                ge(v, s_hc, b, ITS, s - H_RING + 1)
                ge(v, s_carry, b, ITS // 4, (s - H_RING) // 4 + 1)
                v.tensor_tensor_scan(out=h_ring[:, s % H_RING, :], data0=a_ring[:, s % A_RING, :], data1=b_ring[:, s % A_RING, :],
                                     initial=carry[:, q:q + 1], op0=ALU.mult, op1=ALU.add).then_inc(s_scan, 1)

            def gate_chunk(b, k):
                col = (b * BODY + k) * CH
                ge(v, s_red, b, ITS // 4, QUADS * (k + 1))
                ge(v, s_tails, b, 16 * BODY, 16 * (k + 1))
                v.tensor_tensor(tails[:, 0, :], y_bank[:, :], tails[:, 0, :], ALU.mult).then_inc(s_yr, 1)
                ge(v, s_yr, b, BODY, k + 1)
                v.tensor_tensor(u[:, ds(col, CH)], tails[:, 0, :], tails[:, 1, :], ALU.add).then_inc(s_gated, 1)

            def body(b):
                for kind, i, r in ORDER:
                    if kind == "scan":
                        s = i
                        ge(v, s_sel, b, ITS, s + 1)
                        ge(v, s_scan, b, ITS, s - A_RING + 1)
                        v.tensor_tensor(b_ring[:, s % A_RING, :], du_bank[s % 2][:, :],
                                        b_rep[:, ds((b * BODY + s // PAIRS) * CH, CH)], ALU.mult).then_inc(s_bm, 1)
                        if s > 0:
                            scan(b, s - 1)
                        if s == PAIRS + 5:
                            gate_chunk(b, 0)
                    elif r > 0:
                        k = KS * i + r - 1
                        bank = gu_bank[(USES * i + r) % 2]
                        ge(v, s_th, b, BT * KS, k + 1)
                        ge(v, s_o, b, BT * KS, k - 3)
                        v.scalar_tensor_tensor(out=gt[:, k % 2, :], in0=th[:, k % 2, :], scalar=1.0, in1=bank[:, 0:SLOT],
                                               op0=ALU.add, op1=ALU.mult).then_inc(s_gt, 1)
                        ge(v, s_gt, b, BT * KS, k + 1)
                        v.tensor_tensor(hid[:, k % 4, :], gt[:, k % 2, :], bank[:, SLOT:2 * SLOT],
                                        ALU.mult).then_inc(s_hid, 1)
                scan(b, ITS - 1)
                gate_chunk(b, 1)

            bodies(v, body)

            KE = 3
            def add_mamba_rows(c):
                rows = xn[:, ds(c * TC, TC), :]
                v.tensor_tensor(rows, rows, bdn[:, :].unsqueeze(1).broadcast_to([P, TC, D]), ALU.add).then_inc(s_s, 1)
                v.wait_ge(s_dn, c + 1)
                v.wait_ge(s_s, c * KE + 1)
                for k in range(2):
                    half_rows = xn[:, ds(c * TC + 2 * k, 2), :]
                    v.tensor_tensor(half_rows, half_rows, banks[k][:, :].rearrange("p (n c) -> p n c", c=D),
                                    ALU.add).then_inc(s_s, 1)

            chunks(v, add_mamba_rows)
            f = ring[:, 10:12, :].rearrange("p a t -> p (a t)")
            tf = ring[:, 12:14, :].rearrange("p a t -> p (a t)")
            xr = ring[:, 16:18, :].rearrange("p a t -> p (a t)")
            fo = ring[:, 18:20, :].rearrange("p a t -> p (a t)")
            v.wait_ge(s_s, NC * KE)
            for c in range(NC):
                if c > 0:
                    after(v, s_fin, c)
                for n in range(TC):
                    v.wait_ge(s_gs, TC * c + n + 1)
                    g0, g1 = (ring[:, 2 * (2 * (c % 2) + k):2 * (2 * (c % 2) + k) + 2, :].rearrange("p a t -> p (a t)")[:, n * D:(n + 1) * D]
                              for k in range(2))
                    v.scalar_tensor_tensor(out=f[:, n * D:(n + 1) * D], in0=g1, scalar=prob[:, 1, TC * c + n:TC * c + n + 1],
                                           in1=g0, op0=ALU.mult, op1=ALU.add).then_inc(s_f, 1)
                v.wait_ge(s_tf, c + 1)
                v.scalar_tensor_tensor(out=tf, in0=tf, scalar=1.0, in1=f, op0=ALU.add, op1=ALU.mult).then_inc(s_mix, 1)
                v.wait_ge(s_mix, 2 * c + 1)
                v.scalar_tensor_tensor(out=tf, in0=tf, scalar=0.5, in1=xn[:, TC * c:TC * c + TC, :].rearrange("p n c -> p (n c)"),
                                       op0=ALU.mult, op1=ALU.mult).then_inc(s_mix, 1)
                v.wait_ge(s_mix, 2 * c + 2)
                v.wait_ge(s_xr, 16 * (c + 1))
                after(v, s_out, 16 * c)
                v.tensor_tensor(fo, tf, xr, ALU.add).then_inc(s_fin, 1)

        @block.tensor
        def _(pe):
            pe.wait_ge(s_cst, 16 * 21)
            for c in range(NC):
                pe.wait_ge(s_norm, c + 1)
                after(pe, s_trev, c)
                for src, k in ((yh, 0), (xn, 2)):
                    for h in range(2):
                        for n in range(TC):
                            ins = pe.transpose(banks[k + h][:, n * P:(n + 1) * P],
                                               src[:, c * TC + n, h * P:(h + 1) * P],
                                               ident[:, :])
                ins.then_inc(s_tr, 1)
                pe.wait_ge(s_trev, c + 1)
                after(pe, s_lrev, c)
                for m in range(2):
                    for h in range(2):
                        ins = pe.matmul(banks[4 + m][:, :], wup[:, h, m * P:(m + 1) * P], yT[:, h, :], start=(h == 0), stop=(h == 1))
                ins.then_inc(s_lr, 1)
                for n in range(TC):
                    for h in range(2):
                        ins = pe.matmul(banks[6][:, (c * TC + n) * E:(c * TC + n + 1) * E], xT[:, h, n * P:(n + 1) * P], gsb[:, h, :],
                                        start=(h == 0), stop=(h == 1))
                ins.then_inc(s_logit, 1)
            pe.wait_ge(s_cnt, 1)
            pe.wait_ge(s_ones, 1)
            pe.matmul(banks[7][:, 0:256], upper, small(7), start=True, stop=True)
            pe.matmul(banks[7][:, 256:512], ones[:, :], small(7), start=True, stop=True).then_inc(s_cnt, 1)
            def delta_product(c):
                pe.wait_ge(s_u, c + 1)
                after(pe, s_dlt, KD * c)
                pe.matmul(banks[0][:, :], wdl[:, :], u[:, ds(c * CH, CH)], start=True, stop=True).then_inc(s_dp, 1)

            chunks(pe, delta_product)
            def b_and_c_product(c):
                after(pe, s_bcev, 2 * c)
                pe.matmul(banks[1][:, :], wbc[:, 0, :], u[:, ds(c * CH, CH)], start=True, stop=True)
                pe.matmul(banks[2][:, :], wbc[:, 1, :], u[:, ds(c * CH, CH)], start=True, stop=True).then_inc(s_bc, 1)

            chunks(pe, b_and_c_product)
            pe.wait_ge(s_bcev, 2 * NC)
            pe.wait_ge(s_dlt, KD * NC)
            pe.wait_ge(s_slot, 1)
            pe.wait_ge(s_setup, 2)

            def reduce_quad(b, q):
                i = q % QUADS
                ge(pe, s_hc, b, ITS, 4 * q + 4)
                if i == 0:
                    ge(pe, s_yr, b, BODY, q // QUADS)
                for g in range(4):
                    ins = pe.matmul(y_bank[32 * g:32 * g + 32, :], win[:, 30 - 2 * i:62 - 2 * i],
                                    p_ring[:, (4 * q + g) % P_RING, :], start=(i == 0), stop=(i == QUADS - 1),
                                    skip_group_check=True)
                ins.then_inc(s_red, 1)

            def expert_out(b, k):
                i, r = k // KS, k % KS
                ge(pe, s_hid, b, BT * KS, k + 1)
                if r == 0:
                    ge(pe, s_oev, b, BT, i)
                for s in range(2):
                    ins = pe.matmul(o_bank[:, s * D:(s + 1) * D], hid[:, k % 4, s * P:(s + 1) * P],
                                    wring[:, k % W_RING, 4 * P:WROW], start=(r == 0 and s == 0), stop=(r == KS - 1),
                                    skip_group_check=True)
                ins.then_inc(s_o, 1)

            def body(b):
                for kind, i, r in ORDER:
                    if kind == "scan":
                        s = i
                        g, i16 = s % 4, (s % PAIRS) // 4
                        jl = (g * QUADS + i16) % 32
                        par = s // PAIRS
                        if s % PAIRS == 0:
                            ge(pe, s_stack[par], b, 32, 32)
                        ge(pe, s_exp, b, ITS, s - 1)
                        pe.matmul(dl_bank[s % 2][:, :], pick[:, jl, :], stack[:, par, 0, g // 2, :], start=True, stop=True)
                        ge(pe, s_bm, b, ITS, s - 1)
                        pe.matmul(du_bank[s % 2][:, :], pick[:, jl, :], stack[:, par, 1, g // 2, :], start=True,
                                  stop=True).then_inc(s_sel, 1)
                        if s % 4 == 3 and s >= 7:
                            reduce_quad(b, s // 4 - 1)
                    elif r == 0:
                        ge(pe, s_xg[i % 2], b, 16 * BT // 2, 16 * (i // 2 + 1))
                        ge(pe, s_hid, b, BT * KS, KS * i - 1)
                        for h in range(2):
                            for s in range(2):
                                ins = pe.transpose(gu_bank[(USES * i) % 2][:, h * SLOT + s * P:h * SLOT + s * P + P],
                                                   xg[:, 0, s, h * P:(h + 1) * P], ident[:, :])
                        ins.then_inc(s_gu, 1)
                        if i > 0:
                            expert_out(b, KS * i - 1)
                    else:
                        k = KS * i + r - 1
                        bank = gu_bank[(USES * i + r) % 2]
                        ge(pe, s_xgT, b, BT, i + 1)
                        ge(pe, s_hid, b, BT * KS, KS * i if r <= 2 else k - 1)
                        ge(pe, s_w[k % W_RING], b, 32 * (BT * KS // W_RING), 32 * (k // W_RING + 1))
                        for m in range(2):
                            for h in range(2):
                                ins = pe.matmul(bank[:, m * SLOT:(m + 1) * SLOT],
                                                wring[:, k % W_RING, (2 * m + h) * P:(2 * m + h + 1) * P],
                                                xgT[:, i % 2, h, :], start=(h == 0), stop=(h == 1))
                        ins.then_inc(s_gu, 1)
                        if r > 1:
                            expert_out(b, k - 1)
                reduce_quad(b, ITS // 4 - 1)
                expert_out(b, BT * KS - 1)

            bodies(pe, body)
            pe.wait_ge(s_gated, NC)
            for c in range(NC):
                after(pe, s_s, 3 * c)
                for n in range(TC):
                    ins = pe.matmul(banks[n // 2][:, (n % 2) * D:(n % 2 + 1) * D], u[:, c * CH + n * P:c * CH + (n + 1) * P], wdn[:, :],
                                    start=True, stop=True)
                ins.then_inc(s_dn, 1)


def kernel(**inputs):
    import concourse.bacc as bacc
    from concourse.bass_utils import run_bass_kernel_spmd as run

    a = {k: np.ascontiguousarray(v) for k, v in inputs.items()}
    at, ff = "L0_attn_", "L0_ffn_"

    def cols(v, n):
        return np.ascontiguousarray(v.reshape(n, P).T)

    pq = np.arange(P)
    w1 = a[ff + "experts_w1"].reshape(E, 2, P, KS, P).transpose(0, 3, 2, 1, 4)
    w3 = a[ff + "experts_w3"].reshape(E, 2, P, KS, P).transpose(0, 3, 2, 1, 4)
    arrays = dict(
        x=a[at + "x"], gam=cols(a[at + "ln_gamma"], 2), bet=cols(a[at + "ln_beta"], 2), w_up=a[at + "W_up"],
        b_up=cols(a[at + "b_up"], 2), conv_w=a[at + "conv_w"].reshape(P, 3), conv_b=a[at + "conv_b"].reshape(P, 1),
        w_dl=a[at + "W_delta"], b_dl=a[at + "b_delta"].reshape(P, 1),
        w_b2=np.concatenate([a[at + "W_B"]] * 2, 1), w_c2=np.concatenate([a[at + "W_C"]] * 2, 1),
        a_log=np.ascontiguousarray(a[at + "A_log"].reshape(4, QUADS, 2, N).transpose(2, 3, 1, 0).reshape(P, PAIRS)),
        dvec=a[at + "D"].reshape(P, 1), w_dn=a[at + "W_down"], b_dn=a[at + "b_down"], gate=a[ff + "gate"],
        w13=np.ascontiguousarray(np.stack([w1, w3], 3).reshape(E * KS, P, 4 * P)),
        w2=a[ff + "experts_w2"].reshape(E * KS, P, D),
        c_ident=np.eye(P, dtype=np.float32), c_upper=np.triu(np.ones((P, P), np.float32), 1),
        c_pick=(pq[:, None] % 64 == np.arange(64)[None, :]).astype(np.float32),
        c_win=(np.arange(62)[None, :] == 30 + pq[:, None] // 64).astype(np.float32),
        c_first=np.tile(np.arange(E, 0, -1, dtype=np.float32), (P, 1)),
        c_start=np.tile(np.arange(TILES, dtype=np.float32) * SLOT, (P, 1)),
    )
    nc = bacc.Bacc("TRN2", target_bir_lowering=False, num_devices=1)
    args = [nc.dram_tensor(f"in_{k}", v.shape, F32, kind="ExternalInput").ap() for k, v in arrays.items()]
    out = nc.dram_tensor("out", (1, T, D), F32, kind="ExternalOutput").ap()
    mamba_and_experts(nc, *args, out)
    r = run(nc, [{f"in_{k}": v for k, v in arrays.items()}], core_ids=[0])
    return r.results[0]["out"]
```

```python
from contextlib import ExitStack

import numpy as np
import concourse.bass as bass
from concourse import mybir

P = 128
T, D, E, I, N = 4096, 256, 8, 1024, 64
NT = T // P
CH = 512
NC = T // CH
TC = CH // P
PAIRS = P // 2
QUADS = PAIRS // 4
SLOT = 256
SH = SLOT // P
TILES = 2 * T // SLOT + E
KS = I // P
WROW = 2 * 2 * P + D
ROW = D + 2
BODY = 2
BODIES = NC // BODY
AHEAD = BODY
LATE = AHEAD
ITS = BODY * PAIRS
BT = TILES // BODIES
PADS = 2 * SH
TR = 4
H_RING, P_RING, A_RING, B_RING = 8, 8, 4, 2
YH_RING = 6
EPS = 1e-5

F32, F32R, I32, U32 = mybir.dt.float32, mybir.dt.float32r, mybir.dt.int32, mybir.dt.uint32
ALU, ACT, AX = mybir.AluOpType, mybir.ActivationFunctionType, mybir.AxisListType
ds = bass.ds

assert TILES % BODIES == 0 and BT % 2 == 0


def body_turns():
    turns = []
    for i in range(BT):
        for k in range(KS):
            if k == TR:
                turns.append(("rows", i + 1, 0))
            turns.append(("step", i, k))
    for j in range(BODY):
        for n, kind in enumerate(("delta", "b", "c")):
            turns.insert(HALF_TURNS * j + 14 + 3 * n, (kind, j, 0))
    return turns


HALF_TURNS = (BT * (KS + 1) + 3 * BODY) // BODY
TURNS = body_turns()
FIRST_SCAN = dict(conv=11, tanh=15, silu=16, log=20, clip=20, b=24, c=28, split=23, store=34)


def body_order():
    order, done, late = [], 0, None
    for s in range(ITS):
        order.append(("mult", s, 0))
        if late is not None:
            order.append(("gate", late, 0))
        order.append(("scan", s, 0))
        if late is not None:
            order.append(("hid", late, 0))
        late = None
        if done < (s + 1) * len(TURNS) // ITS:
            order.append(("turn", done, 0))
            late = done if TURNS[done][0] == "step" else None
            done += 1
        for name, parts in (("conv", 3), ("silu", 3), ("clip", 1), ("log", 2), ("split", 9), ("store", 1)):
            at = s % PAIRS - FIRST_SCAN[name]
            if 0 <= at < parts:
                order.append((name, s // PAIRS, at))
    return order + [("gate", late, 0), ("hid", late, 0)]


def mamba_and_experts(nc, x, gam, bet, w_up, b_up, conv_w, conv_b, w_dl, b_dl, w_b2, w_c2, a_log,
                      dvec, w_dn, b_dn, gate, w_all, c_ident, c_upper, c_pick, c_win, c_first,
                      c_start, c_token, out):
    with ExitStack() as ctx:
        def sb(name, shape, dt=F32):
            return ctx.enter_context(nc.sbuf_tensor(name, shape, dt))

        def sem(name):
            return ctx.enter_context(nc.semaphore(name))

        x_sorted = nc.dram_tensor("x_sorted", [(TILES + 2) * SLOT, ROW], F32).ap()
        results = nc.dram_tensor("results", [2 * T + PADS * P, D], F32).ap()
        parts_d = nc.dram_tensor("parts_d", [2, 2, P, T], F32).ap()
        tails_d = nc.dram_tensor("tails_d", [P, 2, T], F32).ap()

        xn = sb("xn", [P, NT, ROW])
        b_rep = sb("b_rep", [P, T])
        c_rep = sb("c_rep", [P, NC, CH + 2])
        spare = sb("spare", [P, 7, CH])
        c_now = sb("c_now", [P, BODY, CH])
        wring = sb("wring", [P, KS, WROW])
        arena = sb("arena", [P, (H_RING + P_RING + A_RING + B_RING) * CH])
        stack = sb("stack", [P, 2, 2, 2, CH], F32R)
        pick = sb("pick", [P, 32, P], F32R)
        tails = sb("tails", [P, 2, CH])
        carry = sb("carry", [P, PAIRS])
        a_neg = sb("a_neg", [P, PAIRS])
        xg = sb("xg", [P, SH, D])
        goal = sb("goal", [P, BT, SH, 2])
        xgT = sb("xgT", [P, 2, 2, SLOT])
        o_sb = sb("o_sb", [P, SH, D])
        th = sb("th", [P, 2, SLOT])
        gt = sb("gt", [P, SLOT])
        hid = sb("hid", [P, 4, SLOT])
        ident = sb("ident", [P, P])
        ones = sb("ones", [P, P])
        win = sb("win", [P, 62])
        first = sb("first", [P, E])
        start = sb("start", [P, TILES])
        token = sb("token", [P, NT])
        wdl = sb("wdl", [P, P])
        wbc = sb("wbc", [P, 2, P])
        wdn = sb("wdn", [P, D])
        gsb = sb("gsb", [P, 2, E])
        vec = sb("vec", [P, 12])
        half = sb("half", [P, 5])
        bdn = sb("bdn", [P, D])
        row_i = sb("row_i", [P, TILES], I32)
        new_i = sb("new_i", [P, TILES], I32)
        wup = hid[:, 0:2, :]
        upper, cpick = hid[:, 2, 0:P], hid[:, 2, P:P + 64]
        yh = wring[:, :, :].rearrange("p k c -> p (k c)").rearrange("p (n c) -> p n c", c=D)
        gated = tails[:, 0, :]
        colsT = (c_now, tails)

        ring = arena[:, :].rearrange("p (r t) -> p r t", t=CH)
        h_ring, p_ring = ring[:, 0:H_RING, :], ring[:, H_RING:H_RING + P_RING, :]
        a_ring = ring[:, H_RING + P_RING:H_RING + P_RING + A_RING, :]
        b_ring = ring[:, H_RING + P_RING + A_RING:, :]
        pad_rows = arena[:, 0:PADS * ROW].rearrange("p (v c) -> p v c", c=ROW)
        stat = ring[:, 14, 0:6 * NT].rearrange("p (n k) -> p n k", k=6)
        mv = ring[:, 14, 192:192 + 2 * NT].rearrange("p (n k) -> p n k", k=2)
        rs, ve, root = (ring[:, 14, 256 + NT * k:256 + NT * (k + 1)] for k in range(3))

        prob, slot_i, dest_i = (ring[:, 15, 2 * NT * k:2 * NT * (k + 1)].rearrange("p (k n) -> p k n", k=2) for k in range(3))
        slot_i, dest_i = slot_i.bitcast(U32), dest_i.bitcast(U32)

        def small(k, n=NT * E):
            return ring[:, 16 + k // 2, (k % 2) * 256:(k % 2) * 256 + n]

        def stage(k, name):
            at = dict(cv=0, dlt=0, hilo3=0, thl=1, ud=1, thr=2, sr=2, u=3, hilo2=3, ex=4, hilo0=4, ln=5, hilo1=5,
                      wm=6, du=6)[name]
            return spare[:, at, :] if k == LATE else ring[:, 7 * k + at, :]

        def of_chunk(rep, c, at):
            return rep[:, :, :].rearrange("p c t -> p (c t)")[:, ds(c * (CH + 2) + at, CH)]

        def rows_of(slot):
            return ring[:, slot:slot + 2, :].rearrange("p a t -> p (a t)").rearrange("p (n c) -> p n c", c=D)

        banks = [ctx.enter_context(nc.psum_tensor(f"bank{i}", [P, 512], F32)) for i in range(8)]
        dl_bank, du_bank, y_bank = banks[0:2], banks[2:4], banks[4]
        gu_bank, o_bank = banks[5:7], banks[7]
        u_banks = ((banks[0], banks[2], banks[3]), (banks[1], banks[2], banks[3]),
                   [gu_bank[TURNS.index((kind, 0, 0)) % 2] for kind in ("delta", "b", "c")])
        rows_bank = gu_bank[TURNS.index(("rows", BT, 0)) % 2]

        s_x = [sem(f"s_x{i}") for i in range(4)]
        s_cst, s_pad, s_ones, s_pre = (sem(k) for k in ("s_cst", "s_pad", "s_ones", "s_pre"))
        s_setup, s_aneg, s_norm1, s_norm2, s_stat, s_root = (sem(k) for k in ("s_setup", "s_aneg", "s_norm1", "s_norm2", "s_stat", "s_root"))
        s_xtr, s_xev, s_ytr, s_yev = (sem(k) for k in ("s_xtr", "s_xev", "s_ytr", "s_yev"))
        s_lr, s_lrev, s_logit = (sem(k) for k in ("s_lr", "s_lrev", "s_logit"))
        s_rt, s_rex, s_rex2, s_cnt, s_slot, s_scat, s_meta = (sem(k) for k in ("s_rt", "s_rex", "s_rex2", "s_cnt", "s_slot", "s_scat", "s_meta"))
        s_cvs, s_cv, s_tanh, s_u, s_ud = (sem(k) for k in ("s_cvs", "s_cv", "s_tanh", "s_u", "s_ud"))
        s_dp, s_bc, s_bcev, s_sp, s_dlt = (sem(k) for k in ("s_dp", "s_bc", "s_bcev", "s_sp", "s_dlt"))
        s_partd = [sem(f"s_partd{k}") for k in range(AHEAD + 1)]
        s_stack = [sem("s_stack0"), sem("s_stack1")]
        s_tails, s_sel, s_exp, s_bm, s_scan = (sem(k) for k in ("s_tails", "s_sel", "s_exp", "s_bm", "s_scan"))
        s_carry, s_cnow, s_hc, s_red, s_gt2, s_gated = (sem(k) for k in ("s_carry", "s_cnow", "s_hc", "s_red", "s_gt2", "s_gated"))
        s_dn, s_add, s_bias = (sem(k) for k in ("s_dn", "s_add", "s_bias"))
        s_w = [sem(f"s_w{i}") for i in range(KS)]
        s_xg, s_tr = sem("s_xg"), sem("s_tr")
        s_gu, s_xgT, s_th, s_gt, s_hid = (sem(k) for k in ("s_gu", "s_xgT", "s_th", "s_gt", "s_hid"))
        s_o, s_oev = sem("s_o"), sem("s_oev")
        s_res = sem("s_res")
        s_ld = [sem("s_ld0"), sem("s_ld1")]
        s_st = [sem("s_st0"), sem("s_st1")]
        s_f, s_tf, s_mix, s_fin = (sem(k) for k in ("s_f", "s_tf", "s_mix", "s_fin"))

        ORDER = body_order()
        CONSTS = 22
        KD = 7
        STORES = 16 * 10

        def ge(eng, s, b, per_body, n):
            if isinstance(b, int) and b * per_body + n <= 0:
                return
            eng.wait_ge(s, b * per_body + n)

        def bodies(eng, body):
            body(0, ORDER)
            with eng.Fori(1, BODIES - 1) as b:
                body(b, ORDER)
            body(BODIES - 1, [o for o in ORDER if o[0] not in FIRST_SCAN
                              and not (o[0] == "turn" and TURNS[o[1]][0] in ("delta", "b", "c"))])

        def begun(b):
            return not isinstance(b, int) or b > 0

        def coming(b, j):
            return b * BODY + AHEAD + j

        def in_pairs(eng, step):
            for c in range(2):
                step(c, c)
            with eng.Fori(1, NC // 2 - 1) as p:
                for k in range(2):
                    step(2 * p + k, k)
            for c in range(NC - 2, NC):
                step(c, c % 2)

        def after(eng, s, n):
            if not isinstance(n, int) or n > 0:
                eng.wait_ge(s, n)

        def half_of(c, k):
            return c // 2 if isinstance(c, int) else (c - k) // 2

        block = ctx.enter_context(nc.Block())

        @block.sync
        def _(sp):
            for q in range(4):
                sp.dma_start(xn[:, 8 * q:8 * q + 8, 0:D],
                             x[0, 1024 * q:1024 * q + 1024, :].rearrange("(n p) c -> p n c", p=P)).then_inc(s_x[q], 16)
            for dst, src in ((ident[:, :], c_ident), (upper, c_upper), (win[:, :], c_win),
                             (first[:, :], c_first), (start[:, :], c_start), (cpick, c_pick), (token[:, :], c_token),
                             (wup, w_up.rearrange("(h p) c -> p h c", p=P)), (wdl[:, :], w_dl),
                             (wbc[:, 0, :], w_b2), (wbc[:, 1, :], w_c2), (wdn[:, :], w_dn),
                             (gsb[:, :, :], gate.rearrange("(h p) e -> p h e", p=P)), (a_neg[:, :], a_log),
                             (vec[:, 0:2], gam), (vec[:, 2:4], bet), (vec[:, 4:6], b_up),
                             (vec[:, 6:9], conv_w), (vec[:, 9:10], conv_b), (vec[:, 10:11], b_dl),
                             (vec[:, 11:12], dvec), (bdn[:, :], b_dn.partition_broadcast(P))):
                sp.dma_start(dst, src).then_inc(s_cst, 16)
            sp.wait_ge(s_pad, 2)
            for k in range(PADS):
                sp.dma_start(x_sorted.rearrange("(q v p) c -> v p q c", p=P, v=PADS)[k],
                             pad_rows[:, k, :].unsqueeze(1).broadcast_to([P, (TILES + 2) * SH // PADS, ROW])).then_inc(s_pre, 16)

            def store_parts(c, k):
                sp.wait_ge(s_dlt, (c + 1) * KD)
                for q in range(2):
                    for j in range(2):
                        for h in range(2):
                            sp.dma_start(parts_d[q, h, 64 * j:64 * j + 64, ds(c * CH, CH)],
                                         stage(k, f"hilo{2 * q + j}")[64 * h:64 * h + 64, :]).then_inc(s_partd[k], 16)
                sp.dma_start(tails_d[:, 0, ds(c * CH, CH)], stage(k, "sr")).then_inc(s_partd[k], 16)
                sp.dma_start(tails_d[:, 1, ds(c * CH, CH)], stage(k, "ud")).then_inc(s_partd[k], 16)

            for c in range(AHEAD):
                store_parts(c, c)

            def load_stack(b, k):
                if isinstance(b, int) and b == 0:
                    sp.wait_ge(s_partd[k], STORES)
                else:
                    sp.wait_ge(s_partd[LATE], STORES * (BODY * (b - 1) + k + 1))
                for q in range(2):
                    sp.dma_start(stack[:, k, q, :, :].bitcast(F32),
                                 parts_d[q, :, :, ds((b * BODY + k) * CH, CH)].rearrange("h p t -> p h t")
                                 ).then_inc(s_stack[k], 16)

            def body(b, order):
                ge(sp, s_sel, b, ITS, -PAIRS)
                load_stack(b, 0)
                for kind, i, r in order:
                    if kind == "scan" and i == 8:
                        ge(sp, s_sel, b, ITS, 0)
                        load_stack(b, 1)
                    if kind == "scan" and i % PAIRS == 16:
                        k = i // PAIRS
                        ge(sp, s_add, b, 2 * BODY, 2 * k)
                        sp.dma_start(tails[:, :, :], tails_d[:, :, ds((b * BODY + k) * CH, CH)]).then_inc(s_tails, 16)
                    if kind == "store":
                        store_parts(coming(b, i), LATE)
                    if kind == "turn" and TURNS[i][0] == "step" and TURNS[i][2] == 0:
                        i = TURNS[i][1]
                        row = sp.value_load(row_i[0:1, ds(b * BT + i, 1)], min_val=0, max_val=(E - 1) * KS)
                        new = sp.value_load(new_i[0:1, ds(b * BT + i, 1)], min_val=0, max_val=1)
                        with sp.If(new > 0):
                            for k in range(KS):
                                ge(sp, s_o, b, BT * KS, KS * (i - 1) + k + 1)
                                sp.dma_start(wring[:, k, :], w_all[ds(row + k, 1), :, :].rearrange("a p c -> p (a c)")
                                             ).then_inc(s_w[k], 16)
                        with sp.Else():
                            for k in range(KS):
                                ge(sp, s_o, b, BT * KS, KS * (i - 1) + k + 1)
                                sp.sem_inc(s_w[k], 16)

            bodies(sp, body)
            sp.wait_ge(s_gated, NC)
            sp.wait_ge(s_carry, NC * QUADS)
            sp.wait_ge(s_partd[LATE], STORES * (NC - AHEAD))
            sp.wait_ge(s_res, 16 * SH * TILES)

            def load_rows(c, k):
                after(sp, s_fin, c - 1)
                sp.dma_start(rows_of(6 * k), results[ds(c * CH, CH), :].rearrange("(n p) c -> p n c", p=P)).then_inc(s_ld[k], 16)
                sp.dma_start(rows_of(6 * k + 2), results[ds(c * CH + T, CH), :].rearrange("(n p) c -> p n c", p=P)).then_inc(s_ld[k], 16)
                sp.dma_start(rows_of(6 * k + 4), x[0, ds(c * CH, CH), :].rearrange("(n p) c -> p n c", p=P)).then_inc(s_ld[k], 16)

            load_rows(0, 0)
            load_rows(1, 1)

            def store_out(c, k):
                sp.wait_ge(s_fin, c + 1)
                sp.dma_start(out[0, ds(c * CH, CH), :].rearrange("(n p) c -> p n c", p=P), rows_of(16 + 2 * k)).then_inc(s_st[k], 16)
                if not (isinstance(c, int) and c + 2 >= NC):
                    load_rows(c + 2, k)

            in_pairs(sp, store_out)
            for k in range(2):
                sp.wait_ge(s_st[k], 16 * NC // 2)

        @block.gpsimd
        def _(pool):
            pool.wait_ge(s_slot, 1)
            pool.wait_ge(s_pre, 16 * PADS)
            for k in range(2):
                if k:
                    pool.wait_ge(s_scat, 16 * NT)
                    pool.tensor_copy(xn[:, :, D].bitcast(U32), dest_i[:, 1, :])
                    pool.tensor_copy(xn[:, :, D + 1], prob[:, 1, :]).then_inc(s_meta, 1)
                    pool.wait_ge(s_meta, 1)
                for n in range(NT):
                    pool.indirect_dma_start(x_sorted, bass.IndirectOffsetOnAxis(slot_i[:, k, n:n + 1], 0),
                                            xn[:, n, :], None).then_inc(s_scat, 16)
            pool.wait_ge(s_bcev, 2 * AHEAD)
            pool.wait_ge(s_scat, 16 * 2 * NT)

            def scatter_results(i):
                for s in range(SH):
                    pool.indirect_dma_start(results, bass.IndirectOffsetOnAxis(goal[:, i % BT, s, 0:1].bitcast(U32), 0),
                                            o_sb[:, s, :], None).then_inc(s_res, 16)

            def body(b, order):
                due = None
                for kind, s, r in order:
                    if kind == "turn" and TURNS[s][0] == "step" and TURNS[s][2] == 2 and (TURNS[s][1] > 0 or begun(b)):
                        due = TURNS[s][1] - 1
                    if kind == "scan":
                        k = s // PAIRS
                        if s % PAIRS == 0:
                            pool.tensor_copy(c_now[:, k, :], of_chunk(c_rep, b * BODY + k, 2)).then_inc(s_cnow, 1)
                            ge(pool, s_cnow, b, BODY, k + 1)
                        if s % PAIRS == 32:
                            rows = xn[:, ds((b * BODY + k) * TC, TC), 0:D]
                            pool.tensor_tensor(rows, rows, bdn[:, :].unsqueeze(1).broadcast_to([P, TC, D]), ALU.add
                                               ).then_inc(s_bias, 1)
                        ge(pool, s_scan, b, ITS, s + 1)
                        ge(pool, s_red, b, ITS // 4, (s - P_RING) // 4 + 1)
                        if due is not None:
                            ge(pool, s_oev, b, BT, due + 1)
                        pool.tensor_tensor(p_ring[:, s % P_RING, :], h_ring[:, s % H_RING, :], c_now[:, k, :],
                                           ALU.mult).then_inc(s_hc, 1)
                        if due is not None:
                            scatter_results(due)
                            due = None

            bodies(pool, body)
            pool.wait_ge(s_oev, TILES)
            scatter_results(TILES - 1)

            def add_choices(c, k):
                pool.wait_ge(s_ld[k], 48 * (half_of(c, k) + 1))
                pool.tensor_tensor(rows_of(6 * k), rows_of(6 * k), rows_of(6 * k + 2), ALU.add).then_inc(s_f, 1)

            in_pairs(pool, add_choices)

        @block.scalar
        def _(act):
            act.wait_ge(s_cst, 16 * CONSTS)
            act.activation(a_neg[:, :], a_neg[:, :], ACT.Exp).then_inc(s_aneg, 1)
            act.wait_ge(s_stat, 3)
            act.activation(root, ve, ACT.Sqrt).then_inc(s_root, 1)
            for c in range(NC):
                act.wait_ge(s_xtr, c + 1)
                after(act, s_logit, c - 1)
                for h in range(2):
                    ins = act.activation(colsT[c % 2][:, h, :], banks[2 * (c % 2) + h][:, :], ACT.Copy)
                ins.then_inc(s_xev, 1)
            act.wait_ge(s_stat, 12)
            act.activation(root, ve, ACT.Sqrt).then_inc(s_root, 1)
            act.wait_ge(s_setup, 1)
            for c in range(NC):
                act.wait_ge(s_ytr, c + 1)
                after(act, s_lr, c - 1)
                if c < 2:
                    act.wait_ge(s_logit, NC - 1 + c)
                for h in range(2):
                    ins = act.activation(colsT[c % 2][:, h, :], banks[2 * (c % 2) + h][:, :], ACT.Identity,
                                         bias=vec[:, 2 + h:3 + h], scale=vec[:, h:h + 1])
                ins.then_inc(s_yev, 1)
                act.wait_ge(s_lr, c + 1)
                act.activation(c_rep[:, c, 2:CH + 2], banks[4][:, :], ACT.Identity, bias=vec[:, 4:5])
                if c < NC - 1:
                    act.activation(c_rep[:, c + 1, 0:2], banks[4][:, CH - 2:CH], ACT.Identity, bias=vec[:, 4:5])
                act.activation(b_rep[:, c * CH:(c + 1) * CH], banks[5][:, :], ACT.Identity, bias=half[:, 4:5],
                               scale=0.5).then_inc(s_lrev, 1)
                if c == 1:
                    act.wait_ge(s_rex, 1)
                    act.activation(small(4, NT), small(3, NT), ACT.Exp).then_inc(s_rex2, 1)

            def tanhs(c, k):
                act.activation(stage(k, "thl"), stage(k, "cv"), ACT.Tanh)
                act.activation(stage(k, "thr"), b_rep[:, ds(c * CH, CH)], ACT.Tanh).then_inc(s_tanh, 1)

            def softplus(c, k, part):
                if part == 0:
                    act.wait_ge(s_dp, c + 1)
                    act.activation(stage(k, "ex"), u_banks[k][0][:, :], ACT.Abs, bias=vec[:, 10:11]).then_inc(s_sp, 1)
                elif part == 1:
                    act.wait_ge(s_sp, 3 * c + 1)
                    act.activation(stage(k, "ex"), stage(k, "ex"), ACT.Exp, scale=-1.0).then_inc(s_sp, 1)
                else:
                    act.wait_ge(s_sp, 3 * c + 2)
                    act.activation(stage(k, "ln"), stage(k, "ex"), ACT.Ln, bias=1.0).then_inc(s_sp, 1)

            def wait_for_b_or_c(c, m):
                act.wait_ge(s_bc, 2 * c + m + 1)
                if m == 0:
                    act.wait_ge(s_ud, 2 * c + 1)

            def evict_b_or_c(c, k, m):
                if m == 0:
                    act.activation(b_rep[:, ds(c * CH, CH)], u_banks[k][1][:, :], ACT.Copy).then_inc(s_bcev, 1)
                else:
                    act.activation(of_chunk(c_rep, c, 2), u_banks[k][2][:, :], ACT.Copy).then_inc(s_bcev, 1)

            for c in range(AHEAD):
                act.wait_ge(s_cv, c + 1)
                tanhs(c, c)
            for c in range(AHEAD):
                for part in range(3):
                    softplus(c, c, part)
                for m in range(2):
                    wait_for_b_or_c(c, m)
                    evict_b_or_c(c, c, m)
            for k in range(AHEAD):
                act.wait_ge(s_partd[k], STORES)

            def load_rows(b, i):
                ge(act, s_tr, b, BT, i)
                first_row = b * (BT * SLOT) + i * SLOT
                ge(act, s_res, b, 16 * SH * BT, 16 * SH * (i - BT + 1))
                act.dma_start(xg[:, :, :], x_sorted[ds(first_row, SLOT), 0:D].rearrange("(s p) c -> p s c", p=P)
                              ).then_inc(s_xg, 16)
                act.dma_start(goal[:, i % BT, :, :], x_sorted[ds(first_row, SLOT), D:ROW].rearrange("(s p) c -> p s c", p=P)
                              ).then_inc(s_xg, 16)

            def evict_rows(b, i, bank):
                ge(act, s_tr, b, BT, i + 1)
                act.activation(xgT[:, i % 2, :, :].rearrange("p h t -> p (h t)"), bank[:, :], ACT.Copy).then_inc(s_xgT, 1)

            act.wait_ge(s_scat, 16 * 2 * NT)
            load_rows(0, 0)
            evict_rows(0, 0, rows_bank)
            load_rows(0, 1)

            def evict_out(b, i):
                ge(act, s_o, b, BT * KS, KS * (i + 1))
                ge(act, s_res, b, 16 * SH * BT, 16 * SH * i)
                for s in range(SH):
                    ins = act.activation(o_sb[:, s, :], o_bank[:, s * D:(s + 1) * D], ACT.Identity,
                                         scale=goal[:, i % BT, s, 1:2])
                ins.then_inc(s_oev, 1)

            def save_carry(b, q):
                ge(act, s_scan, b, ITS, 4 * q + 4)
                r, k = (4 * q) % H_RING, q % QUADS
                act.activation(carry[:, 4 * k:4 * k + 4], h_ring[:, r:r + 4, CH - 1], ACT.Copy).then_inc(s_carry, 1)

            def body(b, order):
                with_coming = not (isinstance(b, int) and b == BODIES - 1)
                for kind, i, r in order:
                    if kind == "scan":
                        s, c = i, coming(b, i // PAIRS)
                        work = {FIRST_SCAN[w]: w for w in ("tanh", "b", "c")}.get(s % PAIRS) if with_coming else None
                        if work == "tanh":
                            act.wait_ge(s_cv, c + 1)
                        elif work:
                            wait_for_b_or_c(c, "bc".index(work))
                        ge(act, s_sel, b, ITS, s + 1)
                        ge(act, s_scan, b, ITS, s - A_RING + 1)
                        act.activation(a_ring[:, s % A_RING, :], dl_bank[s % 2][:, :], ACT.Exp,
                                       scale=a_neg[:, s % PAIRS:s % PAIRS + 1]).then_inc(s_exp, 1)
                        if work == "tanh":
                            tanhs(c, LATE)
                        elif work:
                            evict_b_or_c(c, LATE, "bc".index(work))
                        if s % 4 == 1 and (begun(b) or s >= 5):
                            save_carry(b, (s - 5) // 4)
                    elif kind == "log":
                        softplus(coming(b, i), LATE, 1 + r)
                    elif kind == "turn":
                        turn, t, kk = TURNS[i]
                        if turn == "rows":
                            evict_rows(b, t, gu_bank[i % 2])
                            load_rows(b, t + 1)
                        elif turn == "delta":
                            softplus(coming(b, t), LATE, 0)
                        elif turn == "step":
                            k = KS * t + kk
                            ge(act, s_gu, b, BT * KS, k + 1)
                            ge(act, s_gt, b, BT * KS, k - 1)
                            act.activation(th[:, k % 2, :], gu_bank[i % 2][:, 0:SLOT], ACT.Tanh,
                                           scale=0.5).then_inc(s_th, 1)
                            if kk == 1 and (begun(b) or t > 0):
                                evict_out(b, t - 1)

            bodies(act, body)
            save_carry(BODIES, -1)
            evict_out(BODIES, -1)

            def tanh_mix(c, k):
                act.wait_ge(s_f, c + 1)
                after(act, s_fin, c)
                act.activation(rows_of(12), rows_of(6 * k), ACT.Tanh, scale=0.5).then_inc(s_tf, 1)

            in_pairs(act, tanh_mix)
            act.wait_ge(s_xg, 32 * (TILES + 2))

        @block.vector
        def _(v):
            n_st = [0]

            def stat_step(ins):
                n_st[0] += 1
                ins.then_inc(s_stat, 1)
                v.wait_ge(s_stat, n_st[0])

            def inverse_deviation(k):
                stat_step(v.tensor_scalar(ve, mv[:, :, 1], EPS, None, ALU.add))
                v.wait_ge(s_root, k + 1)
                stat_step(v.reciprocal(rs, root))
                stat_step(v.tensor_tensor(root, rs, rs, ALU.mult))
                stat_step(v.tensor_tensor(root, root, ve, ALU.mult))
                stat_step(v.tensor_scalar(root, root, -0.5, 1.5, ALU.mult, ALU.add))
                stat_step(v.tensor_tensor(rs, rs, root, ALU.mult))

            def moments(waits):
                for n in range(NT):
                    if waits and n % 8 == 0:
                        v.wait_ge(s_x[n // 8], 16)
                    ins = v.bn_stats(stat[:, n, :], xn[:, n, 0:D])
                stat_step(ins)
                for n in range(NT):
                    ins = v.bn_aggr(mv[:, n, :], stat[:, n, :])
                stat_step(ins)

            moments(True)
            inverse_deviation(0)
            for n in range(NT):
                ins = v.tensor_scalar(xn[:, n, 0:D], xn[:, n, 0:D], mv[:, n, 0:1], rs[:, n:n + 1], ALU.subtract, ALU.mult)
                if n % TC == TC - 1 and n < NT - 1:
                    ins.then_inc(s_norm1, 1)
            stat_step(ins)
            moments(False)
            inverse_deviation(1)
            for n in range(NT):
                if n >= YH_RING * TC:
                    v.wait_ge(s_ytr, n // TC - YH_RING + 1)
                ins = v.tensor_scalar(yh[:, n % (YH_RING * TC), :], xn[:, n, 0:D], mv[:, n, 0:1], rs[:, n:n + 1],
                                      ALU.subtract, ALU.mult)
                if n % TC == TC - 1:
                    ins.then_inc(s_norm2, 1)

            v.memset(ones[:, :], 1.0).then_inc(s_ones, 1)
            v.memset(pad_rows, 0.0).then_inc(s_pad, 1)
            v.wait_ge(s_cst, 16 * CONSTS)
            v.wait_ge(s_pad, 1)
            for k in range(PADS):
                ins = v.tensor_scalar(pad_rows[:, k, D:D + 1].bitcast(U32), token[:, 0:1], float(2 * T + k * P), None, ALU.add)
            ins.then_inc(s_pad, 1)
            v.memset(carry[:, :], 0.0)
            v.memset(c_rep[:, 0, 0:2], 0.0)
            v.tensor_scalar(half[:, 0:3], vec[:, 6:9], 0.5, None, ALU.mult)
            v.tensor_scalar(half[:, 3:4], vec[:, 9:10], 0.5, None, ALU.mult)
            v.tensor_scalar(half[:, 4:5], vec[:, 5:6], 0.5, None, ALU.mult).then_inc(s_setup, 1)

            n_rt = [0]

            def link(ins):
                n_rt[0] += 1
                ins.then_inc(s_rt, 1)
                v.wait_ge(s_rt, n_rt[0])

            v.wait_ge(s_logit, NC)

            def ne(a):
                return a.rearrange("p (n e) -> p n e", e=E)

            def wide(a):
                return a.unsqueeze(2).broadcast_to([P, NT, E])

            lg, cand, hot1, hot2, msk = small(0), small(1), small(5), small(6), small(7)
            m1, m2, den = small(2, NT), ring[:, 17, 32:64], ring[:, 17, 64:96]
            apart, ratio = small(3, NT), small(4, NT)
            descend = first[:, :].unsqueeze(1).broadcast_to([P, NT, E])
            link(v.tensor_copy(lg, banks[6][:, 0:NT * E]))

            def one_hot(top, hot):
                link(v.tensor_reduce(top, ne(lg), AX.X, ALU.max))
                link(v.tensor_tensor(ne(cand), ne(lg), wide(top), ALU.is_equal))
                link(v.tensor_tensor(ne(cand), ne(cand), descend, ALU.mult))
                link(v.tensor_reduce(den, ne(cand), AX.X, ALU.max))
                link(v.tensor_tensor(ne(hot), ne(cand), wide(den), ALU.is_equal))

            one_hot(m1, hot1)
            link(v.scalar_tensor_tensor(out=lg, in0=hot1, scalar=-3.0e38, in1=lg, op0=ALU.mult, op1=ALU.add))
            one_hot(m2, hot2)
            v.tensor_tensor(apart, m2, m1, ALU.subtract).then_inc(s_rex, 1)
            v.tensor_tensor(msk.rearrange("p (e n) -> p n e", n=NT), ne(hot1), ne(hot2), ALU.add).then_inc(s_cnt, 1)
            link(v.memset(small(11), 1.0))
            incl, excl, slotf, tmp = small(8), small(9), small(10), small(1)
            iv, xv, sv = (a.rearrange("p (e n) -> p e n", n=NT) for a in (incl, excl, slotf))
            cnt, pad, ends, shift, need = (ring[:, 17, 96 + 8 * k:104 + 8 * k] for k in range(5))
            v.wait_ge(s_cnt, 2)
            v.wait_ge(s_ones, 1)
            link(v.tensor_tensor_scan(out=incl, data0=small(11), data1=banks[7][:, 256:512], initial=0.0,
                                      op0=ALU.mult, op1=ALU.add))
            link(v.tensor_tensor(excl, incl, banks[7][:, 256:512], ALU.subtract))
            link(v.tensor_tensor(cnt, iv[:, :, NT - 1], xv[:, :, 0], ALU.subtract))
            te = ring[:, 16, 0:E * TILES].rearrange("p (e t) -> p e t", t=TILES)
            link(v.tensor_tensor(te, start[:, :].unsqueeze(1).broadcast_to([P, E, TILES]),
                                 cnt.unsqueeze(2).broadcast_to([P, E, TILES]), ALU.is_lt))
            link(v.tensor_reduce(need, te, AX.X, ALU.add))
            link(v.tensor_scalar(pad, need, float(SLOT), None, ALU.mult))
            link(v.tensor_tensor_scan(out=ends, data0=ones[:, 0:E], data1=pad, initial=0.0, op0=ALU.mult, op1=ALU.add))
            link(v.tensor_tensor(shift, ends, pad, ALU.subtract))
            link(v.tensor_tensor(shift, shift, xv[:, :, 0], ALU.subtract))
            link(v.tensor_tensor(slotf, excl, banks[7][:, 0:256], ALU.add))
            link(v.tensor_tensor(sv, sv, shift.unsqueeze(2).broadcast_to([P, E, NT]), ALU.add))
            for k, hot in enumerate((hot1, hot2)):
                link(v.tensor_tensor(ne(tmp), ne(hot), slotf.rearrange("p (e n) -> p n e", n=NT), ALU.mult))
                link(v.tensor_reduce(den, ne(tmp), AX.X, ALU.add))
                link(v.tensor_copy(slot_i[:, k, :], den))
            tl = ring[:, 16, 0:TILES * E].rearrange("p (t e) -> p t e", e=E)
            te2, new = ring[:, 16, 400:400 + TILES], ring[:, 16, 450:450 + TILES]
            link(v.tensor_tensor(tl, start[:, :].unsqueeze(2).broadcast_to([P, TILES, E]),
                                 ends.unsqueeze(1).broadcast_to([P, TILES, E]), ALU.is_ge))
            link(v.tensor_reduce(te2, tl, AX.X, ALU.add))
            link(v.tensor_scalar(te2, te2, float(E - 1), float(KS), ALU.min, ALU.mult))
            v.memset(new[:, 0:1], 1.0)
            link(v.tensor_tensor(new[:, 1:TILES], te2[:, 1:TILES], te2[:, 0:TILES - 1], ALU.not_equal))
            v.tensor_copy(row_i[:, :], te2)
            link(v.tensor_copy(new_i[:, :], new))
            v.wait_ge(s_rex2, 1)
            link(v.tensor_scalar(den, ratio, 1.0, None, ALU.add))
            link(v.reciprocal(den, den))
            link(v.tensor_scalar(prob[:, 0, :], den, 0.5, None, ALU.mult))
            v.tensor_tensor(prob[:, 1, :], prob[:, 0, :], ratio, ALU.mult)
            for k in range(2):
                v.tensor_scalar(dest_i[:, k, :], token[:, :], float(k * T), None, ALU.add)
            v.tensor_scalar(xn[:, :, D].bitcast(U32), token[:, :], 0.0, None, ALU.add)
            v.tensor_copy(xn[:, :, D + 1], prob[:, 0, :]).then_inc(s_slot, 1)
            v.wait_ge(s_slot, 1)

            def conv(c, k, tap):
                cv = stage(k, "cv")
                if tap == 0:
                    if k == LATE:
                        after(v, s_partd[LATE], STORES * (c - AHEAD))
                    v.wait_ge(s_lrev, c + 1)
                    v.tensor_scalar(cv, of_chunk(c_rep, c, 2), half[:, 2:3], half[:, 3:4], ALU.mult, ALU.add).then_inc(s_cvs, 1)
                else:
                    v.wait_ge(s_cvs, 2 * c + tap)
                    v.scalar_tensor_tensor(out=cv, in0=of_chunk(c_rep, c, 2 - tap), scalar=half[:, 2 - tap:3 - tap],
                                           in1=cv, op0=ALU.mult, op1=ALU.add).then_inc(s_cvs if tap == 1 else s_cv, 1)

            def silu(c, k, part):
                if part == 0:
                    v.wait_ge(s_tanh, c + 1)
                    v.scalar_tensor_tensor(out=stage(k, "u"), in0=stage(k, "thl"), scalar=1.0, in1=stage(k, "cv"),
                                           op0=ALU.add, op1=ALU.mult).then_inc(s_u, 1)
                elif part == 1:
                    v.scalar_tensor_tensor(out=stage(k, "sr"), in0=stage(k, "thr"), scalar=1.0, in1=b_rep[:, ds(c * CH, CH)],
                                           op0=ALU.add, op1=ALU.mult).then_inc(s_ud, 1)
                else:
                    v.wait_ge(s_u, c + 1)
                    v.wait_ge(s_ud, 2 * c + 1)
                    v.scalar_tensor_tensor(out=stage(k, "ud"), in0=stage(k, "u"), scalar=vec[:, 11:12], in1=stage(k, "sr"),
                                           op0=ALU.mult, op1=ALU.mult).then_inc(s_ud, 1)

            def clip(c, k):
                v.wait_ge(s_sp, 3 * c + 1)
                v.tensor_scalar(stage(k, "dlt"), u_banks[k][0][:, :], vec[:, 10:11], 0.0, ALU.add, ALU.max).then_inc(s_dlt, 1)

            def split(c, k, part):
                dlt, du, wm = stage(k, "dlt"), stage(k, "du"), stage(k, "wm")
                hilo = [stage(k, f"hilo{n}").bitcast(F32R) for n in range(4)]
                base = c * KD
                if part == 0:
                    v.wait_ge(s_sp, 3 * c + 3)
                    v.tensor_scalar(wm, stage(k, "ex"), 1.0, -1.0, ALU.add, ALU.add).then_inc(s_dlt, 1)
                elif part == 1:
                    v.wait_ge(s_dlt, base + 1)
                    v.tensor_tensor(dlt, stage(k, "ln"), dlt, ALU.add)
                elif part == 2:
                    v.wait_ge(s_dlt, base + 2)
                    v.tensor_tensor(wm, wm, stage(k, "ex"), ALU.subtract).then_inc(s_dlt, 1)
                elif part == 3:
                    v.wait_ge(s_dlt, base + 3)
                    v.tensor_tensor(dlt, dlt, wm, ALU.subtract).then_inc(s_dlt, 1)
                elif part == 4:
                    v.wait_ge(s_dlt, base + 4)
                    v.tensor_copy(hilo[0], dlt)
                elif part == 5:
                    v.tensor_tensor(du, dlt, stage(k, "u"), ALU.mult).then_inc(s_dlt, 1)
                elif part == 6:
                    v.wait_ge(s_dlt, base + 5)
                    v.tensor_tensor(hilo[1], dlt, hilo[0].bitcast(F32), ALU.subtract)
                elif part == 7:
                    v.wait_ge(s_bc, 2 * c + 2)
                    v.tensor_copy(hilo[2], du).then_inc(s_dlt, 1)
                else:
                    v.wait_ge(s_dlt, base + 6)
                    v.tensor_tensor(hilo[3], du, hilo[2].bitcast(F32), ALU.subtract).then_inc(s_dlt, 1)

            v.wait_ge(s_pre, 16 * PADS)
            for c in range(AHEAD):
                for tap in range(3):
                    conv(c, c, tap)
            for c in range(AHEAD):
                for part in range(3):
                    silu(c, c, part)
            for c in range(AHEAD):
                clip(c, c)
                for part in range(9):
                    split(c, c, part)
            v.tensor_copy(pick[:, :, :].rearrange("p a (b k) -> p (a b) k", b=2),
                          cpick.unsqueeze(2).broadcast_to([P, 64, 64])).then_inc(s_setup, 1)
            v.wait_ge(s_aneg, 1)
            v.tensor_scalar(a_neg[:, :], a_neg[:, :], -1.0, None, ALU.mult).then_inc(s_setup, 1)
            v.wait_ge(s_bcev, 2 * AHEAD)
            for k in range(AHEAD):
                v.wait_ge(s_partd[k], STORES)

            def scan(b, s):
                q = s % PAIRS
                ge(v, s_exp, b, ITS, s + 1)
                ge(v, s_bm, b, ITS, s + 1)
                ge(v, s_hc, b, ITS, s - H_RING + 1)
                ge(v, s_carry, b, ITS // 4, (s - H_RING) // 4 + 1)
                v.tensor_tensor_scan(out=h_ring[:, s % H_RING, :], data0=a_ring[:, s % A_RING, :],
                                     data1=b_ring[:, s % B_RING, :], initial=carry[:, q:q + 1],
                                     op0=ALU.mult, op1=ALU.add).then_inc(s_scan, 1)

            def gate_chunk(b, k):
                ge(v, s_red, b, ITS // 4, QUADS * (k + 1))
                ge(v, s_tails, b, 16 * BODY, 16 * (k + 1))
                v.tensor_tensor(gated, y_bank[:, :], tails[:, 0, :], ALU.mult).then_inc(s_gt2, 1)
                ge(v, s_gt2, b, BODY, k + 1)
                v.tensor_tensor(gated, gated, tails[:, 1, :], ALU.add).then_inc(s_gated, 1)

            def add_rows(b, k, h):
                ge(v, s_dn, b, 2 * BODY, 2 * k + h + 1)
                ge(v, s_bias, b, BODY, k + 1)
                rows = xn[:, ds((b * BODY + k) * TC + 2 * h, 2), 0:D]
                v.tensor_tensor(rows, rows, y_bank[:, :].rearrange("p (n c) -> p n c", c=D), ALU.add).then_inc(s_add, 1)

            def body(b, order):
                for kind, i, r in order:
                    if kind == "mult":
                        s = i
                        ge(v, s_sel, b, ITS, s + 1)
                        ge(v, s_scan, b, ITS, s - B_RING + 1)
                        v.tensor_tensor(b_ring[:, s % B_RING, :], du_bank[s % 2][:, :],
                                        b_rep[:, ds((b * BODY + s // PAIRS) * CH, CH)], ALU.mult).then_inc(s_bm, 1)
                    elif kind == "scan":
                        s = i
                        if begun(b) or s > 0:
                            scan(b, s - 1)
                        if begun(b) or s >= PAIRS:
                            k = s // PAIRS - 1
                            if s % PAIRS == 5:
                                gate_chunk(b, k)
                            if s % PAIRS in (7, 9):
                                add_rows(b, k, (s % PAIRS) // 2 - 3)
                    elif kind == "conv":
                        conv(coming(b, i), LATE, r)
                    elif kind == "silu":
                        silu(coming(b, i), LATE, r)
                    elif kind == "clip":
                        clip(coming(b, i), LATE)
                    elif kind == "split":
                        split(coming(b, i), LATE, r)
                    elif kind in ("gate", "hid"):
                        _, t, kk = TURNS[i]
                        k = KS * t + kk
                        if kind == "gate":
                            ge(v, s_th, b, BT * KS, k + 1)
                            ge(v, s_hid, b, BT * KS, k)
                            v.scalar_tensor_tensor(out=gt[:, :], in0=th[:, k % 2, :], scalar=1.0,
                                                   in1=gu_bank[i % 2][:, 0:SLOT], op0=ALU.add, op1=ALU.mult).then_inc(s_gt, 1)
                        else:
                            ge(v, s_gt, b, BT * KS, k + 1)
                            ge(v, s_o, b, BT * KS, k - 3)
                            v.tensor_tensor(hid[:, k % 4, :], gt[:, :], gu_bank[i % 2][:, SLOT:2 * SLOT],
                                            ALU.mult).then_inc(s_hid, 1)

            bodies(v, body)
            scan(BODIES, -1)
            gate_chunk(BODIES, -1)
            add_rows(BODIES, -1, 0)
            add_rows(BODIES, -1, 1)
            v.wait_ge(s_add, 2 * NC)

            def finish(c, k):
                tf = rows_of(12)
                v.wait_ge(s_tf, c + 1)
                v.scalar_tensor_tensor(out=tf, in0=tf, scalar=1.0, in1=rows_of(6 * k), op0=ALU.add, op1=ALU.mult).then_inc(s_mix, 1)
                v.wait_ge(s_mix, 2 * c + 1)
                v.scalar_tensor_tensor(out=tf, in0=tf, scalar=0.5, in1=xn[:, ds(c * TC, TC), 0:D],
                                       op0=ALU.mult, op1=ALU.mult).then_inc(s_mix, 1)
                v.wait_ge(s_mix, 2 * c + 2)
                after(v, s_st[k], 16 * half_of(c, k))
                v.tensor_tensor(rows_of(16 + 2 * k), tf, rows_of(6 * k + 4), ALU.add).then_inc(s_fin, 1)

            in_pairs(v, finish)

        @block.tensor
        def _(pe):
            pe.wait_ge(s_cst, 16 * CONSTS)

            def transpose_chunk(src, n0, c):
                for h in range(2):
                    for n in range(TC):
                        ins = pe.transpose(banks[2 * (c % 2) + h][:, n * P:(n + 1) * P], src[:, n0 + n, h * P:(h + 1) * P],
                                           ident[:, :])
                return ins

            def logits(c):
                pe.wait_ge(s_xev, c + 1)
                for n in range(TC):
                    for h in range(2):
                        ins = pe.matmul(banks[6][:, (c * TC + n) * E:(c * TC + n + 1) * E], colsT[c % 2][:, h, n * P:(n + 1) * P],
                                        gsb[:, h, :], start=(h == 0), stop=(h == 1))
                ins.then_inc(s_logit, 1)

            for c in range(NC):
                if c < NC - 1:
                    pe.wait_ge(s_norm1, c + 1)
                else:
                    pe.wait_ge(s_stat, 9)
                after(pe, s_xev, c - 1)
                transpose_chunk(xn, c * TC, c).then_inc(s_xtr, 1)
                if c > 0:
                    logits(c - 1)
            logits(NC - 1)

            def left_right(c):
                pe.wait_ge(s_yev, c + 1)
                after(pe, s_lrev, c)
                for m in range(2):
                    for h in range(2):
                        ins = pe.matmul(banks[4 + m][:, :], wup[:, h, m * P:(m + 1) * P], colsT[c % 2][:, h, :],
                                        start=(h == 0), stop=(h == 1))
                ins.then_inc(s_lr, 1)

            def counts():
                pe.wait_ge(s_cnt, 1)
                pe.wait_ge(s_ones, 1)
                pe.matmul(banks[7][:, 0:256], upper, small(7), start=True, stop=True)
                pe.matmul(banks[7][:, 256:512], ones[:, :], small(7), start=True, stop=True).then_inc(s_cnt, 1)

            for c in range(NC):
                pe.wait_ge(s_norm2, c + 1)
                after(pe, s_yev, c - 1)
                if c < 2:
                    pe.wait_ge(s_xev, NC - 1 + c)
                transpose_chunk(yh, (c % YH_RING) * TC, c).then_inc(s_ytr, 1)
                if c > 0:
                    left_right(c - 1)
                if c == 3:
                    counts()
            left_right(NC - 1)

            def product(c, k, m):
                if m == 0:
                    pe.wait_ge(s_u, c + 1)
                w = wdl[:, :] if m == 0 else wbc[:, m - 1, :]
                pe.matmul(u_banks[k][m][:, :], w, stage(k, "u"), start=True, stop=True).then_inc(s_bc if m else s_dp, 1)

            pe.wait_ge(s_yev, NC)
            for c in range(AHEAD):
                for m in range(3):
                    if c and m == 1:
                        pe.wait_ge(s_bcev, 2)
                    product(c, c, m)
            pe.wait_ge(s_bcev, 2 * AHEAD)
            pe.wait_ge(s_dlt, KD * AHEAD)
            pe.wait_ge(s_lrev, NC)
            pe.wait_ge(s_setup, 3)

            def reduce_quad(b, q):
                i = q % QUADS
                ge(pe, s_hc, b, ITS, 4 * q + 4)
                if i == 0:
                    ge(pe, s_add, b, 2 * BODY, 2 * (q // QUADS))
                for g in range(4):
                    ins = pe.matmul(y_bank[32 * g:32 * g + 32, :], win[:, 30 - 2 * i:62 - 2 * i],
                                    p_ring[:, (4 * q + g) % P_RING, :], start=(i == 0), stop=(i == QUADS - 1),
                                    skip_group_check=True)
                ins.then_inc(s_red, 1)

            def down(b, k, h):
                ge(pe, s_gated, b, BODY, k + 1)
                if h:
                    ge(pe, s_add, b, 2 * BODY, 2 * k + 1)
                for n in range(2):
                    ins = pe.matmul(y_bank[:, n * D:(n + 1) * D], gated[:, (2 * h + n) * P:(2 * h + n + 1) * P], wdn[:, :],
                                    start=True, stop=True)
                ins.then_inc(s_dn, 1)

            def expert_out(b, k):
                i, r = k // KS, k % KS
                ge(pe, s_hid, b, BT * KS, k + 1)
                if r == 0:
                    ge(pe, s_oev, b, BT, i)
                for s in range(SH):
                    ins = pe.matmul(o_bank[:, s * D:(s + 1) * D], hid[:, k % 4, s * P:(s + 1) * P],
                                    wring[:, r, 4 * P:WROW], start=(r == 0 and s == 0), stop=(r == KS - 1),
                                    skip_group_check=True)
                ins.then_inc(s_o, 1)

            def transpose_rows(b, i, bank):
                ge(pe, s_xg, b, 32 * BT, 32 * (i + 1))
                for h in range(2):
                    for s in range(SH):
                        ins = pe.transpose(bank[:, h * SLOT + s * P:h * SLOT + (s + 1) * P],
                                           xg[:, s, h * P:(h + 1) * P], ident[:, :])
                ins.then_inc(s_tr, 1)

            def bank_free(b, n, last):
                n -= 2
                while last and n >= 0 and TURNS[n][0] in ("delta", "b", "c"):
                    n -= 2
                kind, t, k = TURNS[n]
                if n < 0:
                    t -= BT
                if kind == "step":
                    ge(pe, s_hid, b, BT * KS, KS * t + k + 1)
                elif kind == "rows":
                    ge(pe, s_xgT, b, BT, t + 1)
                elif kind == "delta":
                    pe.wait_ge(s_dlt, KD * coming(b, t) + 1)
                else:
                    pe.wait_ge(s_bcev, 2 * coming(b, t) + 1 + "bc".index(kind))

            def body(b, order):
                last = isinstance(b, int) and b == BODIES - 1
                for kind, i, _ in order:
                    if kind == "scan":
                        s = i
                        g, i16 = s % 4, (s % PAIRS) // 4
                        jl = (g * QUADS + i16) % 32
                        par = s // PAIRS
                        if s % PAIRS == 0:
                            ge(pe, s_stack[par], b, 32, 32)
                        ge(pe, s_exp, b, ITS, s - 1)
                        pe.matmul(dl_bank[s % 2][:, :], pick[:, jl, :], stack[:, par, 0, g // 2, :], start=True, stop=True)
                        ge(pe, s_bm, b, ITS, s - 1)
                        pe.matmul(du_bank[s % 2][:, :], pick[:, jl, :], stack[:, par, 1, g // 2, :], start=True,
                                  stop=True).then_inc(s_sel, 1)
                        at = s % PAIRS
                        if at % 4 == 3 and at != 7 and (begun(b) or s > 3):
                            reduce_quad(b, s // 4 - 1)
                        if at in (6, 8) and (begun(b) or s > PAIRS):
                            down(b, s // PAIRS - 1, at // 2 - 3)
                        if at == 9:
                            reduce_quad(b, s // 4 - 2)
                    elif kind == "turn":
                        turn, t, kk = TURNS[i]
                        k = KS * t + kk
                        if turn == "step" and (begun(b) or k > 1):
                            expert_out(b, k - 2)
                        bank_free(b, i, last)
                        if turn == "rows":
                            transpose_rows(b, t, gu_bank[i % 2])
                        elif turn == "step":
                            if kk == 0:
                                ge(pe, s_xgT, b, BT, t + 1)
                            ge(pe, s_w[kk], b, 16 * BT, 16 * (t + 1))
                            for m in range(2):
                                for h in range(2):
                                    ins = pe.matmul(gu_bank[i % 2][:, m * SLOT:(m + 1) * SLOT],
                                                    wring[:, kk, (2 * m + h) * P:(2 * m + h + 1) * P],
                                                    xgT[:, t % 2, h, :], start=(h == 0), stop=(h == 1))
                            ins.then_inc(s_gu, 1)
                        else:
                            product(coming(b, t), LATE, ("delta", "b", "c").index(turn))

            transpose_rows(0, 0, rows_bank)
            bodies(pe, body)
            reduce_quad(BODIES, -1)
            expert_out(BODIES, -2)
            expert_out(BODIES, -1)
            down(BODIES, -1, 0)
            down(BODIES, -1, 1)


def kernel(**inputs):
    import concourse.bacc as bacc
    from concourse.bass_utils import run_bass_kernel_spmd as run

    a = {k: np.ascontiguousarray(v) for k, v in inputs.items()}
    at, ff = "L0_attn_", "L0_ffn_"

    def cols(v, n):
        return np.ascontiguousarray(v.reshape(n, P).T)

    pq = np.arange(P)
    w1 = a[ff + "experts_w1"].reshape(E, 2, P, KS, P).transpose(0, 3, 2, 1, 4)
    w3 = a[ff + "experts_w3"].reshape(E, 2, P, KS, P).transpose(0, 3, 2, 1, 4)
    arrays = dict(
        x=a[at + "x"], gam=cols(a[at + "ln_gamma"], 2), bet=cols(a[at + "ln_beta"], 2), w_up=a[at + "W_up"],
        b_up=cols(a[at + "b_up"], 2), conv_w=a[at + "conv_w"].reshape(P, 3), conv_b=a[at + "conv_b"].reshape(P, 1),
        w_dl=a[at + "W_delta"], b_dl=a[at + "b_delta"].reshape(P, 1),
        w_b2=np.concatenate([a[at + "W_B"]] * 2, 1), w_c2=np.concatenate([a[at + "W_C"]] * 2, 1),
        a_log=np.ascontiguousarray(a[at + "A_log"].reshape(4, QUADS, 2, N).transpose(2, 3, 1, 0).reshape(P, PAIRS)),
        dvec=a[at + "D"].reshape(P, 1), w_dn=a[at + "W_down"], b_dn=a[at + "b_down"], gate=a[ff + "gate"],
        w_all=np.concatenate([np.stack([w1, w3], 3).reshape(E * KS, P, 4 * P),
                              a[ff + "experts_w2"].reshape(E * KS, P, D)], 2),
        c_ident=np.eye(P, dtype=np.float32), c_upper=np.triu(np.ones((P, P), np.float32), 1),
        c_pick=(pq[:, None] % 64 == np.arange(64)[None, :]).astype(np.float32),
        c_win=(np.arange(62)[None, :] == 30 + pq[:, None] // 64).astype(np.float32),
        c_first=np.tile(np.arange(E, 0, -1, dtype=np.float32), (P, 1)),
        c_start=np.tile(np.arange(TILES, dtype=np.float32) * SLOT, (P, 1)),
        c_token=np.arange(T, dtype=np.float32).reshape(NT, P).T.copy(),
    )
    nc = bacc.Bacc("TRN2", target_bir_lowering=False, num_devices=1)
    args = [nc.dram_tensor(f"in_{k}", v.shape, F32, kind="ExternalInput").ap() for k, v in arrays.items()]
    out = nc.dram_tensor("out", (1, T, D), F32, kind="ExternalOutput").ap()
    mamba_and_experts(nc, *args, out)
    r = run(nc, [{f"in_{k}": v for k, v in arrays.items()}], core_ids=[0])
    return r.results[0]["out"]
```

```python
from contextlib import ExitStack

import numpy as np
import concourse.bass as bass
from concourse import mybir

P = 128
T, D, E, I, N = 4096, 256, 8, 1024, 64
NT = T // P
CH = 512
NC = T // CH
TC = CH // P
PAIRS = P // 2
QUADS = PAIRS // 4
SLOT = 256
SH = SLOT // P
TILES = 2 * T // SLOT + E
KS = I // P
WROW = 2 * 2 * P + D
ROW = D + 2
BODY = 2
BODIES = NC // BODY
AHEAD = BODY
LATE = AHEAD
ITS = BODY * PAIRS
BT = TILES // BODIES
PADS = SH
FULL = 2 * T // SLOT
TR = 4
H_RING, P_RING, A_RING, B_RING = 8, 16, 2, 2
SETS = 4
YH_RING = 6
EPS = 1e-5

F32, F32R, I32, U32 = mybir.dt.float32, mybir.dt.float32r, mybir.dt.int32, mybir.dt.uint32
ALU, ACT, AX = mybir.AluOpType, mybir.ActivationFunctionType, mybir.AxisListType
ds = bass.ds

assert TILES % BODIES == 0 and BT % 2 == 0


def body_turns():
    turns = []
    for i in range(BT):
        for k in range(KS):
            if k == TR:
                turns.append(("rows", i + 1, 0))
            turns.append(("step", i, k))
    for j in range(BODY):
        for n, kind in enumerate(("delta", "b", "c")):
            turns.insert(HALF_TURNS * j + FIRST_TURN + 3 * n, (kind, j, 0))
    return turns


HALF_TURNS = (BT * (KS + 1) + 3 * BODY) // BODY
FIRST_TURN = 14
TURNS = body_turns()
FIRST_SCAN = dict(conv=11, tanh=15, silu=16, log=20, clip=20, b=24, c=28, split=23, store=34)


def body_order():
    order, done, late = [], 0, None
    for s in range(ITS):
        order.append(("mult", s, 0))
        if late is not None:
            order.append(("gate", late, 0))
        order.append(("scan", s, 0))
        if late is not None:
            order.append(("hid", late, 0))
        late = None
        if done < (s + 1) * len(TURNS) // ITS:
            order.append(("turn", done, 0))
            late = done if TURNS[done][0] == "step" else None
            done += 1
        for name, parts in (("conv", 3), ("silu", 3), ("clip", 1), ("log", 2), ("split", 9), ("store", 1)):
            at = s % PAIRS - FIRST_SCAN[name]
            if 0 <= at < parts:
                order.append((name, s // PAIRS, at))
    return order + [("gate", late, 0), ("hid", late, 0)]


def mamba_and_experts(nc, x, gam, bet, w_up, b_up, conv_w, conv_b, w_dl, b_dl, w_b2, w_c2, a_log,
                      dvec, w_dn, b_dn, gate, w_all, c_ident, c_upper, c_pick, c_win, c_first,
                      c_start, c_token, out):
    with ExitStack() as ctx:
        def sb(name, shape, dt=F32):
            return ctx.enter_context(nc.sbuf_tensor(name, shape, dt))

        def sem(name):
            return ctx.enter_context(nc.semaphore(name))

        x_sorted = nc.dram_tensor("x_sorted", [(TILES + 2) * SLOT, ROW], F32).ap()
        results = nc.dram_tensor("results", [2 * T + PADS * P, D], F32).ap()
        parts_d = nc.dram_tensor("parts_d", [4, P, T], F32).ap()
        tails_d = nc.dram_tensor("tails_d", [P, 2, T], F32).ap()

        xn = sb("xn", [P, NT, ROW])
        b_rep = sb("b_rep", [P, T])
        c_rep = sb("c_rep", [P, NC, CH + 2])
        spare = sb("spare", [P, 7, CH])
        c_now = sb("c_now", [P, CH])
        wring = sb("wring", [P, KS, WROW])
        arena = sb("arena", [P, (H_RING + P_RING + A_RING + B_RING) * CH])
        stack = sb("stack", [P, 2, 4, CH], F32R)
        pick = sb("pick", [P, QUADS, P], F32R)
        tails = sb("tails", [P, 2, CH])
        carry = sb("carry", [P, PAIRS])
        a_neg = sb("a_neg", [P, PAIRS])
        xg = sb("xg", [P, SH, D])
        goal = sb("goal", [P, BT, SH, 2])
        xgT = sb("xgT", [P, 2, 2, SLOT])
        o_sb = sb("o_sb", [P, SH, D])
        th = sb("th", [P, SLOT])
        gt = sb("gt", [P, SLOT])
        hid = sb("hid", [P, 4, SLOT])
        ident = sb("ident", [P, P])
        win = sb("win", [P, 62])
        wdl = sb("wdl", [P, P])
        wbc = sb("wbc", [P, 2, P])
        wdn = sb("wdn", [P, D])
        vec = sb("vec", [P, 12])
        half = sb("half", [P, 5])
        bdn = sb("bdn", [P, D])
        row_i = sb("row_i", [P, TILES], I32)
        new_i = sb("new_i", [P, TILES], I32)
        live_i = sb("live_i", [P, TILES], I32)
        wup = hid[:, 0:2, :]
        ones, first, start, token = (hid[:, 3, a:b] for a, b in ((0, P), (P, P + E), (P + E, P + E + TILES),
                                                                 (P + E + TILES, P + E + TILES + NT)))
        gsb = hid[:, 3, 2 * P - 2 * E:2 * P].rearrange("p (h e) -> p h e", h=2)
        upper, cpick = hid[:, 2, 0:P], hid[:, 2, P:P + 32]
        yh = wring[:, :, :].rearrange("p k c -> p (k c)").rearrange("p (n c) -> p n c", c=D)
        gated = tails[:, 0, :]
        colsT = (spare, tails)

        ring = arena[:, :].rearrange("p (r t) -> p r t", t=CH)
        h_ring, p_ring = ring[:, 0:H_RING, :], ring[:, H_RING:H_RING + P_RING, :]
        a_ring = ring[:, H_RING + P_RING:H_RING + P_RING + A_RING, :]
        b_ring = ring[:, H_RING + P_RING + A_RING:, :]
        pad_rows = arena[:, 0:PADS * ROW].rearrange("p (v c) -> p v c", c=ROW)
        stat = ring[:, 14, 0:6 * NT].rearrange("p (n k) -> p n k", k=6)
        mv = ring[:, 14, 192:192 + 2 * NT].rearrange("p (n k) -> p n k", k=2)
        rs, ve, root = (ring[:, 14, 256 + NT * k:256 + NT * (k + 1)] for k in range(3))

        prob, slot_i, dest_i = (ring[:, 15, 2 * NT * k:2 * NT * (k + 1)].rearrange("p (k n) -> p k n", k=2) for k in range(3))
        slot_i, dest_i = slot_i.bitcast(U32), dest_i.bitcast(U32)

        def small(k, n=NT * E):
            return ring[:, 16 + k // 2, (k % 2) * 256:(k % 2) * 256 + n]

        def stage(k, name):
            at = dict(cv=0, dlt=0, hilo3=0, thl=1, ud=1, thr=2, sr=2, u=3, hilo2=3, ex=4, hilo0=4, ln=5, hilo1=5,
                      wm=6, du=6)[name]
            return spare[:, at, :] if k == LATE else ring[:, 7 * k + at, :]

        def of_chunk(rep, c, at):
            return rep[:, :, :].rearrange("p c t -> p (c t)")[:, ds(c * (CH + 2) + at, CH)]

        def rows_of(slot):
            return ring[:, slot:slot + 2, :].rearrange("p a t -> p (a t)").rearrange("p (n c) -> p n c", c=D)

        OUT_AT, TANH_AT = (4 * SETS + 2, 4 * SETS + 4), (4 * SETS, 4 * SETS + 6)
        x_again = [a.rearrange("p (n c) -> p n c", c=D) for k in range(3) for a in (
            b_rep[:, 2 * k * CH:2 * (k + 1) * CH],
            c_rep[:, :, :].rearrange("p c t -> p (c t)")[:, 2 * k * CH:2 * (k + 1) * CH],
            spare[:, 2 * k:2 * k + 2, :].rearrange("p a t -> p (a t)"))]

        banks = [ctx.enter_context(nc.psum_tensor(f"bank{i}", [P, 512], F32)) for i in range(8)]
        dl_bank, du_bank, y_bank = banks[0:2], banks[2:4], banks[4]
        gu_bank, o_bank = banks[5:7], banks[7]
        u_banks = ((banks[0], banks[2], banks[3]), (banks[1], banks[2], banks[3]),
                   [gu_bank[TURNS.index((kind, 0, 0)) % 2] for kind in ("delta", "b", "c")])
        rows_bank = gu_bank[TURNS.index(("rows", BT, 0)) % 2]

        s_x = [sem(f"s_x{i}") for i in range(4)]
        s_first = sem("s_first")
        s_cst, s_pad, s_ones, s_pre = (sem(k) for k in ("s_cst", "s_pad", "s_ones", "s_pre"))
        s_setup, s_aneg, s_norm1, s_norm2, s_stat, s_root = (sem(k) for k in ("s_setup", "s_aneg", "s_norm1", "s_norm2", "s_stat", "s_root"))
        s_xtr, s_xev, s_ytr, s_yev = (sem(k) for k in ("s_xtr", "s_xev", "s_ytr", "s_yev"))
        s_lr, s_lrev, s_logit = (sem(k) for k in ("s_lr", "s_lrev", "s_logit"))
        s_rt, s_rex, s_rex2, s_cnt, s_slot, s_scat, s_meta = (sem(k) for k in ("s_rt", "s_rex", "s_rex2", "s_cnt", "s_slot", "s_scat", "s_meta"))
        s_cvs, s_cv, s_tanh, s_u, s_ud = (sem(k) for k in ("s_cvs", "s_cv", "s_tanh", "s_u", "s_ud"))
        s_dp, s_bc, s_bcev, s_sp, s_dlt = (sem(k) for k in ("s_dp", "s_bc", "s_bcev", "s_sp", "s_dlt"))
        s_partd = [sem(f"s_partd{k}") for k in range(AHEAD + 1)]
        s_stack = [sem("s_stack0"), sem("s_stack1")]
        s_tails, s_sel, s_exp, s_bm, s_scan = (sem(k) for k in ("s_tails", "s_sel", "s_exp", "s_bm", "s_scan"))
        s_carry, s_cnow, s_hc, s_red, s_gt2, s_gated = (sem(k) for k in ("s_carry", "s_cnow", "s_hc", "s_red", "s_gt2", "s_gated"))
        s_dn, s_add, s_bias = (sem(k) for k in ("s_dn", "s_add", "s_bias"))
        s_w = [sem(f"s_w{i}") for i in range(KS)]
        s_xg, s_tr = sem("s_xg"), sem("s_tr")
        s_gu, s_xgT, s_th, s_gt, s_hid = (sem(k) for k in ("s_gu", "s_xgT", "s_th", "s_gt", "s_hid"))
        s_o, s_oev = sem("s_o"), sem("s_oev")
        s_res = sem("s_res")
        s_ld = [sem(f"s_ld{k}") for k in range(SETS)]
        s_again = sem("s_again")
        s_st = [sem("s_st0"), sem("s_st1")]
        s_f, s_tf, s_mix, s_fin = (sem(k) for k in ("s_f", "s_tf", "s_mix", "s_fin"))

        ORDER = body_order()
        CONSTS = 20
        KD = 7
        STORES = 16 * 6

        def ge(eng, s, b, per_body, n):
            if isinstance(b, int) and b * per_body + n <= 0:
                return
            eng.wait_ge(s, b * per_body + n)

        def bodies(eng, body):
            body(0, ORDER)
            with eng.Fori(1, BODIES - 1) as b:
                body(b, ORDER)
            body(BODIES - 1, [o for o in ORDER if o[0] not in FIRST_SCAN
                              and not (o[0] == "turn" and TURNS[o[1]][0] in ("delta", "b", "c"))])

        def begun(b):
            return not isinstance(b, int) or b > 0

        def coming(b, j):
            return b * BODY + AHEAD + j

        def after(eng, s, n):
            if not isinstance(n, int) or n > 0:
                eng.wait_ge(s, n)

        block = ctx.enter_context(nc.Block())

        @block.sync
        def _(sp):
            sp.dma_start(ident[:, :], c_ident).then_inc(s_first, 16)
            sp.dma_start(gsb[:, :, :], gate.rearrange("(h p) e -> p h e", p=P)).then_inc(s_first, 16)
            for q in range(4):
                sp.dma_start(xn[:, 8 * q:8 * q + 8, 0:D],
                             x[0, 1024 * q:1024 * q + 1024, :].rearrange("(n p) c -> p n c", p=P)).then_inc(s_x[q], 16)
            for dst, src in ((upper, c_upper), (win[:, :], c_win),
                             (first[:, :], c_first), (start[:, :], c_start), (cpick, c_pick), (token[:, :], c_token),
                             (wup, w_up.rearrange("(h p) c -> p h c", p=P)), (wdl[:, :], w_dl),
                             (wbc[:, 0, :], w_b2), (wbc[:, 1, :], w_c2), (wdn[:, :], w_dn),
                             (a_neg[:, :], a_log),
                             (vec[:, 0:2], gam), (vec[:, 2:4], bet), (vec[:, 4:6], b_up),
                             (vec[:, 6:9], conv_w), (vec[:, 9:10], conv_b), (vec[:, 10:11], b_dl),
                             (vec[:, 11:12], dvec), (bdn[:, :], b_dn.partition_broadcast(P))):
                sp.dma_start(dst, src).then_inc(s_cst, 16)
            sp.wait_ge(s_pad, 2)
            for k in range(PADS):
                sp.dma_start(x_sorted.rearrange("(q v p) c -> v p q c", p=P, v=PADS)[k],
                             pad_rows[:, k, :].unsqueeze(1).broadcast_to([P, (TILES + 2) * SH // PADS, ROW])).then_inc(s_pre, 16)

            def store_parts(c, k):
                sp.wait_ge(s_dlt, (c + 1) * KD)
                for n in range(4):
                    sp.dma_start(parts_d[n, :, ds(c * CH, CH)], stage(k, f"hilo{n}")).then_inc(s_partd[k], 16)
                sp.dma_start(tails_d[:, 0, ds(c * CH, CH)], stage(k, "sr")).then_inc(s_partd[k], 16)
                sp.dma_start(tails_d[:, 1, ds(c * CH, CH)], stage(k, "ud")).then_inc(s_partd[k], 16)

            for c in range(AHEAD):
                store_parts(c, c)

            def load_stack(b, k):
                if isinstance(b, int) and b == 0:
                    sp.wait_ge(s_partd[k], STORES)
                else:
                    sp.wait_ge(s_partd[LATE], STORES * (BODY * (b - 1) + k + 1))
                for n in range(4):
                    sp.dma_start(stack[32 * n:32 * n + 32, k, :, :].bitcast(F32),
                                 parts_d[n, :, ds((b * BODY + k) * CH, CH)].rearrange("(g c) t -> c g t", c=32)
                                 ).then_inc(s_stack[k], 16)

            def body(b, order):
                ge(sp, s_sel, b, ITS, -PAIRS)
                load_stack(b, 0)
                for kind, i, r in order:
                    if kind == "scan" and i == 8:
                        ge(sp, s_sel, b, ITS, 0)
                        load_stack(b, 1)
                    if kind == "scan" and i % PAIRS == 16:
                        k = i // PAIRS
                        ge(sp, s_add, b, 2 * BODY, 2 * k)
                        sp.dma_start(tails[:, :, :], tails_d[:, :, ds((b * BODY + k) * CH, CH)]).then_inc(s_tails, 16)
                    if kind == "scan" and i == 12 and isinstance(b, int) and b == BODIES - 1:
                        sp.wait_ge(s_bm, ITS * b)
                        sp.wait_ge(s_cnow, BODY * b)
                        sp.wait_ge(s_partd[LATE], STORES * (NC - AHEAD))
                        for c in range(NC):
                            sp.dma_start(x_again[c], x[0, c * CH:(c + 1) * CH, :].rearrange("(n p) c -> p n c", p=P)
                                         ).then_inc(s_again, 16)
                    if kind == "store":
                        store_parts(coming(b, i), LATE)
                    if kind == "turn" and TURNS[i][0] == "step" and TURNS[i][2] == 0:
                        i = TURNS[i][1]
                        row = sp.value_load(row_i[0:1, ds(b * BT + i, 1)], min_val=0, max_val=(E - 1) * KS)
                        new = sp.value_load(new_i[0:1, ds(b * BT + i, 1)], min_val=0, max_val=1)
                        with sp.If(new > 0):
                            for k in range(KS):
                                ge(sp, s_o, b, BT * KS, KS * (i - 1) + k + 1)
                                sp.dma_start(wring[:, k, :], w_all[ds(row + k, 1), :, :].rearrange("a p c -> p (a c)")
                                             ).then_inc(s_w[k], 16)
                        with sp.Else():
                            for k in range(KS):
                                ge(sp, s_o, b, BT * KS, KS * (i - 1) + k + 1)
                                sp.sem_inc(s_w[k], 16)

            bodies(sp, body)
            sp.wait_ge(s_gated, NC)
            sp.wait_ge(s_carry, NC * QUADS)
            sp.wait_ge(s_partd[LATE], STORES * (NC - AHEAD))
            sp.wait_ge(s_res, 16 * SH * TILES)

            def load_results(c):
                k = c % SETS
                after(sp, s_fin, c - SETS + 1)
                for m in range(2):
                    sp.dma_start(rows_of(4 * k + 2 * m),
                                 results[m * T + c * CH:m * T + (c + 1) * CH, :].rearrange("(n p) c -> p n c", p=P)
                                 ).then_inc(s_ld[k], 16)

            for c in range(SETS):
                load_results(c)
            for c in range(NC):
                sp.wait_ge(s_fin, c + 1)
                sp.dma_start(out[0, c * CH:(c + 1) * CH, :].rearrange("(n p) c -> p n c", p=P), rows_of(OUT_AT[c % 2])
                             ).then_inc(s_st[c % 2], 16)
                if c + SETS < NC:
                    load_results(c + SETS)
            for k in range(2):
                sp.wait_ge(s_st[k], 16 * NC // 2)

        @block.gpsimd
        def _(pool):
            pool.wait_ge(s_slot, 1)
            pool.wait_ge(s_pre, 16 * PADS)
            for k in range(2):
                if k:
                    pool.wait_ge(s_scat, 16 * NT)
                    pool.tensor_copy(xn[:, :, D].bitcast(U32), dest_i[:, 1, :])
                    pool.tensor_copy(xn[:, :, D + 1], prob[:, 1, :]).then_inc(s_meta, 1)
                    pool.wait_ge(s_meta, 1)
                for n in range(NT):
                    pool.indirect_dma_start(x_sorted, bass.IndirectOffsetOnAxis(slot_i[:, k, n:n + 1], 0),
                                            xn[:, n, :], None).then_inc(s_scat, 16)
            pool.wait_ge(s_bcev, 2 * AHEAD)
            pool.wait_ge(s_scat, 16 * 2 * NT)

            def scatter_results(i):
                for s in range(SH):
                    pool.indirect_dma_start(results, bass.IndirectOffsetOnAxis(goal[:, i % BT, s, 0:1].bitcast(U32), 0),
                                            o_sb[:, s, :], None).then_inc(s_res, 16)

            def body(b, order):
                due = None
                for kind, s, r in order:
                    if kind == "turn" and TURNS[s][0] == "step" and TURNS[s][2] == 2 and (TURNS[s][1] > 0 or begun(b)):
                        due = TURNS[s][1] - 1
                    if kind == "scan":
                        k = s // PAIRS
                        if s % PAIRS == 0:
                            ge(pool, s_hc, b, ITS, s)
                            pool.tensor_copy(c_now[:, :], of_chunk(c_rep, b * BODY + k, 2)).then_inc(s_cnow, 1)
                            ge(pool, s_cnow, b, BODY, k + 1)
                        if s % PAIRS == 32:
                            rows = xn[:, ds((b * BODY + k) * TC, TC), 0:D]
                            pool.tensor_tensor(rows, rows, bdn[:, :].unsqueeze(1).broadcast_to([P, TC, D]), ALU.add
                                               ).then_inc(s_bias, 1)
                        ge(pool, s_scan, b, ITS, s + 1)
                        ge(pool, s_red, b, ITS // 4, (s - P_RING) // 4 + 1)
                        if due is not None:
                            ge(pool, s_oev, b, BT, due + 1)
                        pool.tensor_tensor(p_ring[:, s % P_RING, :], h_ring[:, s % H_RING, :], c_now[:, :],
                                           ALU.mult).then_inc(s_hc, 1)
                        if due is not None:
                            scatter_results(due)
                            due = None

            bodies(pool, body)
            pool.wait_ge(s_oev, TILES)
            scatter_results(TILES - 1)

            for c in range(NC):
                k = c % SETS
                pool.wait_ge(s_ld[k], 32 * (c // SETS + 1))
                pool.tensor_tensor(rows_of(4 * k), rows_of(4 * k), rows_of(4 * k + 2), ALU.add).then_inc(s_f, 1)

        @block.scalar
        def _(act):
            act.wait_ge(s_stat, 3)
            act.activation(root, ve, ACT.Sqrt).then_inc(s_root, 1)
            for c in range(NC):
                act.wait_ge(s_xtr, c + 1)
                after(act, s_logit, c - 1)
                for h in range(2):
                    ins = act.activation(colsT[c % 2][:, h, :], banks[2 * (c % 2) + h][:, :], ACT.Copy)
                ins.then_inc(s_xev, 1)
                if c == 4:
                    act.wait_ge(s_stat, 12)
                    act.activation(root, ve, ACT.Sqrt).then_inc(s_root, 1)
            act.wait_ge(s_cst, 16 * CONSTS)
            act.activation(a_neg[:, :], a_neg[:, :], ACT.Exp).then_inc(s_aneg, 1)
            def tanhs(c, k):
                act.activation(stage(k, "thl"), stage(k, "cv"), ACT.Tanh)
                act.activation(stage(k, "thr"), b_rep[:, ds(c * CH, CH)], ACT.Tanh).then_inc(s_tanh, 1)

            act.wait_ge(s_setup, 1)
            for c in range(NC):
                act.wait_ge(s_ytr, c + 1)
                after(act, s_lr, c - 1)
                if c < 2:
                    act.wait_ge(s_logit, NC - 1 + c)
                for h in range(2):
                    ins = act.activation(colsT[c % 2][:, h, :], banks[2 * (c % 2) + h][:, :], ACT.Identity,
                                         bias=vec[:, 2 + h:3 + h], scale=vec[:, h:h + 1])
                ins.then_inc(s_yev, 1)
                act.wait_ge(s_lr, c + 1)
                act.activation(c_rep[:, c, 2:CH + 2], banks[4][:, :], ACT.Identity, bias=vec[:, 4:5])
                if c < NC - 1:
                    act.activation(c_rep[:, c + 1, 0:2], banks[4][:, CH - 2:CH], ACT.Identity, bias=vec[:, 4:5])
                act.activation(b_rep[:, c * CH:(c + 1) * CH], banks[5][:, :], ACT.Identity, bias=half[:, 4:5],
                               scale=0.5).then_inc(s_lrev, 1)
                if c == 1:
                    act.wait_ge(s_rex, 1)
                    act.activation(small(4, NT), small(3, NT), ACT.Exp).then_inc(s_rex2, 1)
                if c >= NC - AHEAD:
                    act.wait_ge(s_cv, c - NC + AHEAD + 1)
                    tanhs(c - NC + AHEAD, c - NC + AHEAD)

            def softplus(c, k, part):
                if part == 0:
                    act.wait_ge(s_dp, c + 1)
                    act.activation(stage(k, "ex"), u_banks[k][0][:, :], ACT.Abs, bias=vec[:, 10:11]).then_inc(s_sp, 1)
                elif part == 1:
                    act.wait_ge(s_sp, 3 * c + 1)
                    act.activation(stage(k, "ex"), stage(k, "ex"), ACT.Exp, scale=-1.0).then_inc(s_sp, 1)
                else:
                    act.wait_ge(s_sp, 3 * c + 2)
                    act.activation(stage(k, "ln"), stage(k, "ex"), ACT.Ln, bias=1.0).then_inc(s_sp, 1)

            def wait_for_b_or_c(c, m):
                act.wait_ge(s_bc, 2 * c + m + 1)
                if m == 0:
                    act.wait_ge(s_ud, 2 * c + 1)

            def evict_b_or_c(c, k, m):
                if m == 0:
                    act.activation(b_rep[:, ds(c * CH, CH)], u_banks[k][1][:, :], ACT.Copy).then_inc(s_bcev, 1)
                else:
                    act.activation(of_chunk(c_rep, c, 2), u_banks[k][2][:, :], ACT.Copy).then_inc(s_bcev, 1)

            for c in range(AHEAD):
                for part in range(3):
                    softplus(c, c, part)
                for m in range(2):
                    wait_for_b_or_c(c, m)
                    evict_b_or_c(c, c, m)
            for k in range(AHEAD):
                act.wait_ge(s_partd[k], STORES)

            def load_rows(b, i):
                ge(act, s_tr, b, BT, i)
                first_row = b * (BT * SLOT) + i * SLOT
                ge(act, s_res, b, 16 * SH * BT, 16 * SH * (i - BT + 1))
                act.dma_start(xg[:, :, :], x_sorted[ds(first_row, SLOT), 0:D].rearrange("(s p) c -> p s c", p=P)
                              ).then_inc(s_xg, 16)
                act.dma_start(goal[:, i % BT, :, :], x_sorted[ds(first_row, SLOT), D:ROW].rearrange("(s p) c -> p s c", p=P)
                              ).then_inc(s_xg, 16)

            def evict_rows(b, i, bank):
                ge(act, s_tr, b, BT, i + 1)
                act.activation(xgT[:, i % 2, :, :].rearrange("p h t -> p (h t)"), bank[:, :], ACT.Copy).then_inc(s_xgT, 1)

            act.wait_ge(s_scat, 16 * 2 * NT)
            load_rows(0, 0)
            evict_rows(0, 0, rows_bank)
            load_rows(0, 1)

            def evict_out(b, i):
                ge(act, s_o, b, BT * KS, KS * (i + 1))
                ge(act, s_res, b, 16 * SH * BT, 16 * SH * i)
                for s in range(SH):
                    ins = act.activation(o_sb[:, s, :], o_bank[:, s * D:(s + 1) * D], ACT.Identity,
                                         scale=goal[:, i % BT, s, 1:2])
                ins.then_inc(s_oev, 1)

            def save_carry(b, q):
                ge(act, s_scan, b, ITS, 4 * q + 4)
                r, k = (4 * q) % H_RING, q % QUADS
                act.activation(carry[:, 4 * k:4 * k + 4], h_ring[:, r:r + 4, CH - 1], ACT.Copy).then_inc(s_carry, 1)

            def body(b, order):
                with_coming = not (isinstance(b, int) and b == BODIES - 1)
                for kind, i, r in order:
                    if kind == "scan":
                        s, c = i, coming(b, i // PAIRS)
                        work = {FIRST_SCAN[w]: w for w in ("tanh", "b", "c")}.get(s % PAIRS) if with_coming else None
                        if work == "tanh":
                            act.wait_ge(s_cv, c + 1)
                        elif work:
                            wait_for_b_or_c(c, "bc".index(work))
                        ge(act, s_sel, b, ITS, s + 1)
                        ge(act, s_scan, b, ITS, s - A_RING + 1)
                        act.activation(a_ring[:, s % A_RING, :], dl_bank[s % 2][:, :], ACT.Exp,
                                       scale=a_neg[:, s % PAIRS:s % PAIRS + 1]).then_inc(s_exp, 1)
                        if work == "tanh":
                            tanhs(c, LATE)
                        elif work:
                            evict_b_or_c(c, LATE, "bc".index(work))
                        if s % 4 == 1 and (begun(b) or s >= 5):
                            save_carry(b, (s - 5) // 4)
                    elif kind == "log":
                        softplus(coming(b, i), LATE, 1 + r)
                    elif kind == "turn":
                        turn, t, kk = TURNS[i]
                        if turn == "rows":
                            evict_rows(b, t, gu_bank[i % 2])
                            load_rows(b, t + 1)
                        elif turn == "delta":
                            softplus(coming(b, t), LATE, 0)
                        elif turn == "step":
                            k = KS * t + kk
                            ge(act, s_gu, b, BT * KS, k + 1)
                            ge(act, s_gt, b, BT * KS, k)
                            act.activation(th[:, :], gu_bank[i % 2][:, 0:SLOT], ACT.Tanh,
                                           scale=0.5).then_inc(s_th, 1)
                            if kk == 1 and (begun(b) or t > 0):
                                evict_out(b, t - 1)

            bodies(act, body)
            save_carry(BODIES, -1)
            evict_out(BODIES, -1)

            for c in range(NC):
                act.wait_ge(s_f, c + 1)
                after(act, s_fin, c - 1)
                act.activation(rows_of(TANH_AT[c % 2]), rows_of(4 * (c % SETS)), ACT.Tanh, scale=0.5).then_inc(s_tf, 1)
            act.wait_ge(s_xg, 32 * (TILES + 2))

        @block.vector
        def _(v):
            n_st = [0]

            def stat_step(ins):
                n_st[0] += 1
                ins.then_inc(s_stat, 1)
                v.wait_ge(s_stat, n_st[0])

            def inverse_deviation(k):
                stat_step(v.tensor_scalar(ve, mv[:, :, 1], EPS, None, ALU.add))
                v.wait_ge(s_root, k + 1)
                stat_step(v.reciprocal(rs, root))
                stat_step(v.tensor_tensor(root, rs, rs, ALU.mult))
                stat_step(v.tensor_tensor(root, root, ve, ALU.mult))
                stat_step(v.tensor_scalar(root, root, -0.5, 1.5, ALU.mult, ALU.add))
                stat_step(v.tensor_tensor(rs, rs, root, ALU.mult))

            def moments(waits):
                for n in range(NT):
                    if waits and n % 8 == 0:
                        v.wait_ge(s_x[n // 8], 16)
                    ins = v.bn_stats(stat[:, n, :], xn[:, n, 0:D])
                stat_step(ins)
                for n in range(NT):
                    ins = v.bn_aggr(mv[:, n, :], stat[:, n, :])
                stat_step(ins)

            moments(True)
            inverse_deviation(0)
            for n in range(NT):
                ins = v.tensor_scalar(xn[:, n, 0:D], xn[:, n, 0:D], mv[:, n, 0:1], rs[:, n:n + 1], ALU.subtract, ALU.mult)
                if n % TC == TC - 1 and n < NT - 1:
                    ins.then_inc(s_norm1, 1)
            stat_step(ins)
            v.memset(ones[:, :], 1.0).then_inc(s_ones, 1)
            v.memset(pad_rows, 0.0).then_inc(s_pad, 1)
            v.wait_ge(s_cst, 16 * CONSTS)
            v.wait_ge(s_pad, 1)
            for k in range(PADS):
                ins = v.tensor_scalar(pad_rows[:, k, D:D + 1].bitcast(U32), token[:, 0:1], float(2 * T + k * P), None, ALU.add)
            ins.then_inc(s_pad, 1)
            v.memset(carry[:, :], 0.0)
            v.memset(c_rep[:, 0, 0:2], 0.0)
            v.tensor_scalar(half[:, 0:3], vec[:, 6:9], 0.5, None, ALU.mult)
            v.tensor_scalar(half[:, 3:4], vec[:, 9:10], 0.5, None, ALU.mult)
            v.tensor_scalar(half[:, 4:5], vec[:, 5:6], 0.5, None, ALU.mult).then_inc(s_setup, 1)

            moments(False)
            inverse_deviation(1)
            for n in range(NT):
                if n >= YH_RING * TC:
                    v.wait_ge(s_ytr, n // TC - YH_RING + 1)
                ins = v.tensor_scalar(yh[:, n % (YH_RING * TC), :], xn[:, n, 0:D], mv[:, n, 0:1], rs[:, n:n + 1],
                                      ALU.subtract, ALU.mult)
                if n % TC == TC - 1:
                    ins.then_inc(s_norm2, 1)

            n_rt = [0]

            def link(ins):
                n_rt[0] += 1
                ins.then_inc(s_rt, 1)
                v.wait_ge(s_rt, n_rt[0])

            v.wait_ge(s_logit, NC)

            def ne(a):
                return a.rearrange("p (n e) -> p n e", e=E)

            def wide(a):
                return a.unsqueeze(2).broadcast_to([P, NT, E])

            lg, cand, hot1, hot2, msk = small(0), small(1), small(5), small(6), small(7)
            m1, m2, den = small(2, NT), ring[:, 17, 32:64], ring[:, 17, 64:96]
            apart, ratio = small(3, NT), small(4, NT)
            descend = first[:, :].unsqueeze(1).broadcast_to([P, NT, E])
            link(v.tensor_copy(lg, banks[6][:, 0:NT * E]))

            def one_hot(top, hot):
                link(v.tensor_reduce(top, ne(lg), AX.X, ALU.max))
                link(v.tensor_tensor(ne(cand), ne(lg), wide(top), ALU.is_equal))
                link(v.tensor_tensor(ne(cand), ne(cand), descend, ALU.mult))
                link(v.tensor_reduce(den, ne(cand), AX.X, ALU.max))
                link(v.tensor_tensor(ne(hot), ne(cand), wide(den), ALU.is_equal))

            one_hot(m1, hot1)
            link(v.scalar_tensor_tensor(out=lg, in0=hot1, scalar=-3.0e38, in1=lg, op0=ALU.mult, op1=ALU.add))
            one_hot(m2, hot2)
            v.tensor_tensor(apart, m2, m1, ALU.subtract).then_inc(s_rex, 1)
            v.tensor_tensor(msk.rearrange("p (e n) -> p n e", n=NT), ne(hot1), ne(hot2), ALU.add).then_inc(s_cnt, 1)
            link(v.memset(small(11), 1.0))
            incl, excl, slotf, tmp = small(8), small(9), small(10), small(1)
            iv, xv, sv = (a.rearrange("p (e n) -> p e n", n=NT) for a in (incl, excl, slotf))
            cnt, pad, ends, shift, need = (ring[:, 17, 96 + 8 * k:104 + 8 * k] for k in range(5))
            v.wait_ge(s_cnt, 2)
            v.wait_ge(s_ones, 1)
            link(v.tensor_tensor_scan(out=incl, data0=small(11), data1=banks[7][:, 256:512], initial=0.0,
                                      op0=ALU.mult, op1=ALU.add))
            link(v.tensor_tensor(excl, incl, banks[7][:, 256:512], ALU.subtract))
            link(v.tensor_tensor(cnt, iv[:, :, NT - 1], xv[:, :, 0], ALU.subtract))
            te = ring[:, 16, 0:E * TILES].rearrange("p (e t) -> p e t", t=TILES)
            link(v.tensor_tensor(te, start[:, :].unsqueeze(1).broadcast_to([P, E, TILES]),
                                 cnt.unsqueeze(2).broadcast_to([P, E, TILES]), ALU.is_lt))
            link(v.tensor_reduce(need, te, AX.X, ALU.add))
            link(v.tensor_scalar(pad, need, float(SLOT), None, ALU.mult))
            link(v.tensor_tensor_scan(out=ends, data0=ones[:, 0:E], data1=pad, initial=0.0, op0=ALU.mult, op1=ALU.add))
            link(v.tensor_tensor(shift, ends, pad, ALU.subtract))
            link(v.tensor_tensor(shift, shift, xv[:, :, 0], ALU.subtract))
            link(v.tensor_tensor(slotf, excl, banks[7][:, 0:256], ALU.add))
            link(v.tensor_tensor(sv, sv, shift.unsqueeze(2).broadcast_to([P, E, NT]), ALU.add))
            for k, hot in enumerate((hot1, hot2)):
                link(v.tensor_tensor(ne(tmp), ne(hot), slotf.rearrange("p (e n) -> p n e", n=NT), ALU.mult))
                link(v.tensor_reduce(den, ne(tmp), AX.X, ALU.add))
                link(v.tensor_copy(slot_i[:, k, :], den))
            tl = ring[:, 16, 0:TILES * E].rearrange("p (t e) -> p t e", e=E)
            te2, new = ring[:, 16, 400:400 + TILES], ring[:, 16, 450:450 + TILES]
            link(v.tensor_tensor(tl, start[:, :].unsqueeze(2).broadcast_to([P, TILES, E]),
                                 ends.unsqueeze(1).broadcast_to([P, TILES, E]), ALU.is_ge))
            link(v.tensor_reduce(te2, tl, AX.X, ALU.add))
            link(v.tensor_scalar(new, te2, float(E), None, ALU.is_lt))
            link(v.tensor_copy(live_i[:, :], new))
            link(v.tensor_scalar(te2, te2, float(E - 1), float(KS), ALU.min, ALU.mult))
            v.memset(new[:, 0:1], 1.0)
            link(v.tensor_tensor(new[:, 1:TILES], te2[:, 1:TILES], te2[:, 0:TILES - 1], ALU.not_equal))
            v.tensor_copy(row_i[:, :], te2)
            link(v.tensor_copy(new_i[:, :], new))
            v.wait_ge(s_rex2, 1)
            link(v.tensor_scalar(den, ratio, 1.0, None, ALU.add))
            link(v.reciprocal(den, den))
            link(v.tensor_scalar(prob[:, 0, :], den, 0.5, None, ALU.mult))
            v.tensor_tensor(prob[:, 1, :], prob[:, 0, :], ratio, ALU.mult)
            for k in range(2):
                v.tensor_scalar(dest_i[:, k, :], token[:, :], float(k * T), None, ALU.add)
            v.tensor_scalar(xn[:, :, D].bitcast(U32), token[:, :], 0.0, None, ALU.add)
            v.tensor_copy(xn[:, :, D + 1], prob[:, 0, :]).then_inc(s_slot, 1)
            v.wait_ge(s_slot, 1)

            def conv(c, k, tap):
                cv = stage(k, "cv")
                if tap == 0:
                    if k == LATE:
                        after(v, s_partd[LATE], STORES * (c - AHEAD))
                    v.wait_ge(s_lrev, c + 1)
                    v.tensor_scalar(cv, of_chunk(c_rep, c, 2), half[:, 2:3], half[:, 3:4], ALU.mult, ALU.add).then_inc(s_cvs, 1)
                else:
                    v.wait_ge(s_cvs, 2 * c + tap)
                    v.scalar_tensor_tensor(out=cv, in0=of_chunk(c_rep, c, 2 - tap), scalar=half[:, 2 - tap:3 - tap],
                                           in1=cv, op0=ALU.mult, op1=ALU.add).then_inc(s_cvs if tap == 1 else s_cv, 1)

            def silu(c, k, part):
                if part == 0:
                    v.wait_ge(s_tanh, c + 1)
                    v.scalar_tensor_tensor(out=stage(k, "u"), in0=stage(k, "thl"), scalar=1.0, in1=stage(k, "cv"),
                                           op0=ALU.add, op1=ALU.mult).then_inc(s_u, 1)
                elif part == 1:
                    v.scalar_tensor_tensor(out=stage(k, "sr"), in0=stage(k, "thr"), scalar=1.0, in1=b_rep[:, ds(c * CH, CH)],
                                           op0=ALU.add, op1=ALU.mult).then_inc(s_ud, 1)
                else:
                    v.wait_ge(s_u, c + 1)
                    v.wait_ge(s_ud, 2 * c + 1)
                    v.scalar_tensor_tensor(out=stage(k, "ud"), in0=stage(k, "u"), scalar=vec[:, 11:12], in1=stage(k, "sr"),
                                           op0=ALU.mult, op1=ALU.mult).then_inc(s_ud, 1)

            def clip(c, k):
                v.wait_ge(s_sp, 3 * c + 1)
                v.tensor_scalar(stage(k, "dlt"), u_banks[k][0][:, :], vec[:, 10:11], 0.0, ALU.add, ALU.max).then_inc(s_dlt, 1)

            def split(c, k, part):
                dlt, du, wm = stage(k, "dlt"), stage(k, "du"), stage(k, "wm")
                hilo = [stage(k, f"hilo{n}").bitcast(F32R) for n in range(4)]
                base = c * KD
                if part == 0:
                    v.wait_ge(s_sp, 3 * c + 3)
                    v.tensor_scalar(wm, stage(k, "ex"), 1.0, -1.0, ALU.add, ALU.add).then_inc(s_dlt, 1)
                elif part == 1:
                    v.wait_ge(s_dlt, base + 1)
                    v.tensor_tensor(dlt, stage(k, "ln"), dlt, ALU.add)
                elif part == 2:
                    v.wait_ge(s_dlt, base + 2)
                    v.tensor_tensor(wm, wm, stage(k, "ex"), ALU.subtract).then_inc(s_dlt, 1)
                elif part == 3:
                    v.wait_ge(s_dlt, base + 3)
                    v.tensor_tensor(dlt, dlt, wm, ALU.subtract).then_inc(s_dlt, 1)
                elif part == 4:
                    v.wait_ge(s_dlt, base + 4)
                    v.tensor_copy(hilo[0], dlt)
                elif part == 5:
                    v.tensor_tensor(du, dlt, stage(k, "u"), ALU.mult).then_inc(s_dlt, 1)
                elif part == 6:
                    v.wait_ge(s_dlt, base + 5)
                    v.tensor_tensor(hilo[1], dlt, hilo[0].bitcast(F32), ALU.subtract)
                elif part == 7:
                    v.wait_ge(s_bc, 2 * c + 2)
                    v.tensor_copy(hilo[2], du).then_inc(s_dlt, 1)
                else:
                    v.wait_ge(s_dlt, base + 6)
                    v.tensor_tensor(hilo[3], du, hilo[2].bitcast(F32), ALU.subtract).then_inc(s_dlt, 1)

            v.wait_ge(s_pre, 16 * PADS)
            for c in range(AHEAD):
                for tap in range(3):
                    conv(c, c, tap)
            for c in range(AHEAD):
                for part in range(3):
                    silu(c, c, part)
            for c in range(AHEAD):
                clip(c, c)
                for part in range(9):
                    split(c, c, part)
            v.tensor_copy(pick[:, :, :].rearrange("p a (b k) -> p (a b) k", b=2),
                          cpick.unsqueeze(2).broadcast_to([P, 32, 64])).then_inc(s_setup, 1)
            v.wait_ge(s_aneg, 1)
            v.tensor_scalar(a_neg[:, :], a_neg[:, :], -1.0, None, ALU.mult).then_inc(s_setup, 1)
            v.wait_ge(s_bcev, 2 * AHEAD)
            for k in range(AHEAD):
                v.wait_ge(s_partd[k], STORES)

            def scan(b, s):
                q = s % PAIRS
                ge(v, s_exp, b, ITS, s + 1)
                ge(v, s_bm, b, ITS, s + 1)
                ge(v, s_hc, b, ITS, s - H_RING + 1)
                ge(v, s_carry, b, ITS // 4, (s - H_RING) // 4 + 1)
                v.tensor_tensor_scan(out=h_ring[:, s % H_RING, :], data0=a_ring[:, s % A_RING, :],
                                     data1=b_ring[:, s % B_RING, :], initial=carry[:, q:q + 1],
                                     op0=ALU.mult, op1=ALU.add).then_inc(s_scan, 1)

            def gate_chunk(b, k):
                ge(v, s_red, b, ITS // 4, QUADS * (k + 1))
                ge(v, s_tails, b, 16 * BODY, 16 * (k + 1))
                v.tensor_tensor(gated, y_bank[:, :], tails[:, 0, :], ALU.mult).then_inc(s_gt2, 1)
                ge(v, s_gt2, b, BODY, k + 1)
                v.tensor_tensor(gated, gated, tails[:, 1, :], ALU.add).then_inc(s_gated, 1)

            def add_rows(b, k, h):
                ge(v, s_dn, b, 2 * BODY, 2 * k + h + 1)
                ge(v, s_bias, b, BODY, k + 1)
                rows = xn[:, ds((b * BODY + k) * TC + 2 * h, 2), 0:D]
                v.tensor_tensor(rows, rows, y_bank[:, :].rearrange("p (n c) -> p n c", c=D), ALU.add).then_inc(s_add, 1)

            def body(b, order):
                for kind, i, r in order:
                    if kind == "mult":
                        s = i
                        ge(v, s_sel, b, ITS, s + 1)
                        ge(v, s_scan, b, ITS, s - B_RING + 1)
                        v.tensor_tensor(b_ring[:, s % B_RING, :], du_bank[s % 2][:, :],
                                        b_rep[:, ds((b * BODY + s // PAIRS) * CH, CH)], ALU.mult).then_inc(s_bm, 1)
                    elif kind == "scan":
                        s = i
                        if begun(b) or s > 0:
                            scan(b, s - 1)
                        if begun(b) or s >= PAIRS:
                            k = s // PAIRS - 1
                            if s % PAIRS == 5:
                                gate_chunk(b, k)
                            if s % PAIRS in (7, 9):
                                add_rows(b, k, (s % PAIRS) // 2 - 3)
                    elif kind == "conv":
                        conv(coming(b, i), LATE, r)
                    elif kind == "silu":
                        silu(coming(b, i), LATE, r)
                    elif kind == "clip":
                        clip(coming(b, i), LATE)
                    elif kind == "split":
                        split(coming(b, i), LATE, r)
                    elif kind in ("gate", "hid"):
                        _, t, kk = TURNS[i]
                        k = KS * t + kk
                        if kind == "gate":
                            ge(v, s_th, b, BT * KS, k + 1)
                            ge(v, s_hid, b, BT * KS, k)
                            v.scalar_tensor_tensor(out=gt[:, :], in0=th[:, :], scalar=1.0,
                                                   in1=gu_bank[i % 2][:, 0:SLOT], op0=ALU.add, op1=ALU.mult).then_inc(s_gt, 1)
                        else:
                            ge(v, s_gt, b, BT * KS, k + 1)
                            ge(v, s_o, b, BT * KS, k - 3)
                            v.tensor_tensor(hid[:, k % 4, :], gt[:, :], gu_bank[i % 2][:, SLOT:2 * SLOT],
                                            ALU.mult).then_inc(s_hid, 1)

            bodies(v, body)
            scan(BODIES, -1)
            gate_chunk(BODIES, -1)
            add_rows(BODIES, -1, 0)
            add_rows(BODIES, -1, 1)
            v.wait_ge(s_add, 2 * NC)

            v.wait_ge(s_again, 16 * NC)
            for c in range(NC):
                tf, mix = rows_of(TANH_AT[c % 2]), rows_of(4 * (c % SETS))
                v.wait_ge(s_tf, c + 1)
                v.scalar_tensor_tensor(out=tf, in0=tf, scalar=1.0, in1=mix, op0=ALU.add, op1=ALU.mult).then_inc(s_mix, 1)
                v.wait_ge(s_mix, 2 * c + 1)
                v.scalar_tensor_tensor(out=tf, in0=tf, scalar=0.5, in1=xn[:, c * TC:(c + 1) * TC, 0:D],
                                       op0=ALU.mult, op1=ALU.mult).then_inc(s_mix, 1)
                v.wait_ge(s_mix, 2 * c + 2)
                after(v, s_st[c % 2], 16 * (c // 2))
                v.tensor_tensor(rows_of(OUT_AT[c % 2]), tf, x_again[c], ALU.add).then_inc(s_fin, 1)

        @block.tensor
        def _(pe):
            pe.wait_ge(s_first, 32)

            def transpose_chunk(src, n0, c):
                for h in range(2):
                    for n in range(TC):
                        ins = pe.transpose(banks[2 * (c % 2) + h][:, n * P:(n + 1) * P], src[:, n0 + n, h * P:(h + 1) * P],
                                           ident[:, :])
                return ins

            def logits(c):
                pe.wait_ge(s_xev, c + 1)
                for n in range(TC):
                    for h in range(2):
                        ins = pe.matmul(banks[6][:, (c * TC + n) * E:(c * TC + n + 1) * E], colsT[c % 2][:, h, n * P:(n + 1) * P],
                                        gsb[:, h, :], start=(h == 0), stop=(h == 1))
                ins.then_inc(s_logit, 1)

            for c in range(NC):
                if c < NC - 1:
                    pe.wait_ge(s_norm1, c + 1)
                else:
                    pe.wait_ge(s_stat, 9)
                after(pe, s_xev, c - 1)
                transpose_chunk(xn, c * TC, c).then_inc(s_xtr, 1)
                if c > 0:
                    logits(c - 1)
            logits(NC - 1)

            pe.wait_ge(s_cst, 16 * CONSTS)

            def left_right(c):
                pe.wait_ge(s_yev, c + 1)
                after(pe, s_lrev, c)
                for m in range(2):
                    for h in range(2):
                        ins = pe.matmul(banks[4 + m][:, :], wup[:, h, m * P:(m + 1) * P], colsT[c % 2][:, h, :],
                                        start=(h == 0), stop=(h == 1))
                ins.then_inc(s_lr, 1)

            def counts():
                pe.wait_ge(s_cnt, 1)
                pe.wait_ge(s_ones, 1)
                pe.matmul(banks[7][:, 0:256], upper, small(7), start=True, stop=True)
                pe.matmul(banks[7][:, 256:512], ones[:, :], small(7), start=True, stop=True).then_inc(s_cnt, 1)

            for c in range(NC):
                pe.wait_ge(s_norm2, c + 1)
                after(pe, s_yev, c - 1)
                if c < 2:
                    pe.wait_ge(s_xev, NC - 1 + c)
                transpose_chunk(yh, (c % YH_RING) * TC, c).then_inc(s_ytr, 1)
                if c > 0:
                    left_right(c - 1)
                if c == 1:
                    counts()
            left_right(NC - 1)

            def product(c, k, m):
                if m == 0:
                    pe.wait_ge(s_u, c + 1)
                w = wdl[:, :] if m == 0 else wbc[:, m - 1, :]
                pe.matmul(u_banks[k][m][:, :], w, stage(k, "u"), start=True, stop=True).then_inc(s_bc if m else s_dp, 1)

            pe.wait_ge(s_yev, NC)
            for c in range(AHEAD):
                for m in range(3):
                    if c and m == 1:
                        pe.wait_ge(s_bcev, 2)
                    product(c, c, m)
            pe.wait_ge(s_bcev, 2 * AHEAD)
            pe.wait_ge(s_dlt, KD * AHEAD)
            pe.wait_ge(s_lrev, NC)
            pe.wait_ge(s_setup, 3)

            live = {}

            def if_live(b, t, products, bank, done):
                t, b = t % BT, b + t // BT
                if not isinstance(b, int) or b * BT + t < FULL:
                    products().then_inc(done, 1)
                    return
                tile = b * BT + t
                if tile not in live:
                    live[tile] = pe.value_load(live_i[0:1, tile:tile + 1], min_val=0, max_val=1)
                with pe.If(live[tile] > 0):
                    products().then_inc(done, 1)
                with pe.Else():
                    pe.matmul(bank[:, 0:2], ident[:, :], ident[:, 0:2], start=True, stop=True).then_inc(done, 1)

            def reduce_quad(b, q):
                i = q % QUADS
                ge(pe, s_hc, b, ITS, 4 * q + 4)
                if i == 0:
                    ge(pe, s_add, b, 2 * BODY, 2 * (q // QUADS))
                for g in range(4):
                    ins = pe.matmul(y_bank[32 * g:32 * g + 32, :], win[:, 30 - 2 * i:62 - 2 * i],
                                    p_ring[:, (4 * q + g) % P_RING, :], start=(i == 0), stop=(i == QUADS - 1),
                                    skip_group_check=True)
                ins.then_inc(s_red, 1)

            def down(b, k, h):
                ge(pe, s_gated, b, BODY, k + 1)
                if h:
                    ge(pe, s_add, b, 2 * BODY, 2 * k + 1)
                for n in range(2):
                    ins = pe.matmul(y_bank[:, n * D:(n + 1) * D], gated[:, (2 * h + n) * P:(2 * h + n + 1) * P], wdn[:, :],
                                    start=True, stop=True)
                ins.then_inc(s_dn, 1)

            def expert_out(b, k):
                i, r = k // KS, k % KS
                ge(pe, s_hid, b, BT * KS, k + 1)
                if r == 0:
                    ge(pe, s_oev, b, BT, i)

                def products():
                    for s in range(SH):
                        ins = pe.matmul(o_bank[:, s * D:(s + 1) * D], hid[:, k % 4, s * P:(s + 1) * P],
                                        wring[:, r, 4 * P:WROW], start=(r == 0 and s == 0), stop=(r == KS - 1),
                                        skip_group_check=True)
                    return ins

                if_live(b, i, products, o_bank, s_o)

            def transpose_rows(b, i, bank):
                ge(pe, s_xg, b, 32 * BT, 32 * (i + 1))

                def products():
                    for h in range(2):
                        for s in range(SH):
                            ins = pe.transpose(bank[:, h * SLOT + s * P:h * SLOT + (s + 1) * P],
                                               xg[:, s, h * P:(h + 1) * P], ident[:, :])
                    return ins

                if isinstance(b, int) and b * BT + i == TILES:
                    products().then_inc(s_tr, 1)
                else:
                    if_live(b, i, products, bank, s_tr)

            def spread(b, s):
                g, i16, par = s % 4, (s % PAIRS) // 4, s // PAIRS
                if s % PAIRS == 0:
                    ge(pe, s_stack[par], b, 64, 64)
                ge(pe, s_exp, b, ITS, s - 1)
                ge(pe, s_bm, b, ITS, s - 1)
                for rows, bank in ((slice(0, 64), dl_bank), (slice(64, P), du_bank)):
                    ins = pe.matmul(bank[s % 2][:, :], pick[rows, i16, :], stack[rows, par, g, :], start=True, stop=True)
                ins.then_inc(s_sel, 1)

            def bank_free(b, n, last):
                n -= 2
                while last and n >= 0 and TURNS[n][0] in ("delta", "b", "c"):
                    n -= 2
                kind, t, k = TURNS[n]
                if n < 0:
                    t -= BT
                if kind == "step":
                    ge(pe, s_hid, b, BT * KS, KS * t + k + 1)
                elif kind == "rows":
                    ge(pe, s_xgT, b, BT, t + 1)
                elif kind == "delta":
                    pe.wait_ge(s_dlt, KD * coming(b, t) + 1)
                else:
                    pe.wait_ge(s_bcev, 2 * coming(b, t) + 1 + "bc".index(kind))

            def body(b, order):
                last = isinstance(b, int) and b == BODIES - 1
                for kind, i, _ in order:
                    if kind == "scan":
                        s = i
                        if s % 4 or s == 0:
                            spread(b, s)
                        at = s % PAIRS
                        if at % 4 == 3 and at != 7 and (begun(b) or s > 3):
                            reduce_quad(b, s // 4 - 1)
                        if at in (6, 8) and (begun(b) or s > PAIRS):
                            down(b, s // PAIRS - 1, at // 2 - 3)
                        if at == 9:
                            reduce_quad(b, s // 4 - 2)
                        if s % 4 == 3 and s < ITS - 1:
                            spread(b, s + 1)
                    elif kind == "turn":
                        turn, t, kk = TURNS[i]
                        k = KS * t + kk
                        if turn == "step" and (begun(b) or k > 1):
                            expert_out(b, k - 2)
                        bank_free(b, i, last)
                        if turn == "rows":
                            transpose_rows(b, t, gu_bank[i % 2])
                        elif turn == "step":
                            if kk == 0:
                                ge(pe, s_xgT, b, BT, t + 1)
                            ge(pe, s_w[kk], b, 16 * BT, 16 * (t + 1))

                            def products():
                                for m in range(2):
                                    for h in range(2):
                                        ins = pe.matmul(gu_bank[i % 2][:, m * SLOT:(m + 1) * SLOT],
                                                        wring[:, kk, (2 * m + h) * P:(2 * m + h + 1) * P],
                                                        xgT[:, t % 2, h, :], start=(h == 0), stop=(h == 1))
                                return ins

                            if_live(b, t, products, gu_bank[i % 2], s_gu)
                        else:
                            product(coming(b, t), LATE, ("delta", "b", "c").index(turn))

            transpose_rows(0, 0, rows_bank)
            bodies(pe, body)
            reduce_quad(BODIES, -1)
            expert_out(BODIES, -2)
            expert_out(BODIES, -1)
            down(BODIES, -1, 0)
            down(BODIES, -1, 1)


def kernel(**inputs):
    import concourse.bacc as bacc
    from concourse.bass_utils import run_bass_kernel_spmd as run

    a = {k: np.ascontiguousarray(v) for k, v in inputs.items()}
    at, ff = "L0_attn_", "L0_ffn_"

    def cols(v, n):
        return np.ascontiguousarray(v.reshape(n, P).T)

    pq = np.arange(P)
    w1 = a[ff + "experts_w1"].reshape(E, 2, P, KS, P).transpose(0, 3, 2, 1, 4)
    w3 = a[ff + "experts_w3"].reshape(E, 2, P, KS, P).transpose(0, 3, 2, 1, 4)
    arrays = dict(
        x=a[at + "x"], gam=cols(a[at + "ln_gamma"], 2), bet=cols(a[at + "ln_beta"], 2), w_up=a[at + "W_up"],
        b_up=cols(a[at + "b_up"], 2), conv_w=a[at + "conv_w"].reshape(P, 3), conv_b=a[at + "conv_b"].reshape(P, 1),
        w_dl=a[at + "W_delta"], b_dl=a[at + "b_delta"].reshape(P, 1),
        w_b2=np.concatenate([a[at + "W_B"]] * 2, 1), w_c2=np.concatenate([a[at + "W_C"]] * 2, 1),
        a_log=np.ascontiguousarray(a[at + "A_log"].reshape(4, QUADS, 2, N).transpose(2, 3, 1, 0).reshape(P, PAIRS)),
        dvec=a[at + "D"].reshape(P, 1), w_dn=a[at + "W_down"], b_dn=a[at + "b_down"], gate=a[ff + "gate"],
        w_all=np.concatenate([np.stack([w1, w3], 3).reshape(E * KS, P, 4 * P),
                              a[ff + "experts_w2"].reshape(E * KS, P, D)], 2),
        c_ident=np.eye(P, dtype=np.float32), c_upper=np.triu(np.ones((P, P), np.float32), 1),
        c_pick=(pq[:, None] % 32 == np.arange(32)[None, :]).astype(np.float32),
        c_win=(np.arange(62)[None, :] == 30 + pq[:, None] // 64).astype(np.float32),
        c_first=np.tile(np.arange(E, 0, -1, dtype=np.float32), (P, 1)),
        c_start=np.tile(np.arange(TILES, dtype=np.float32) * SLOT, (P, 1)),
        c_token=np.arange(T, dtype=np.float32).reshape(NT, P).T.copy(),
    )
    nc = bacc.Bacc("TRN2", target_bir_lowering=False, num_devices=1)
    args = [nc.dram_tensor(f"in_{k}", v.shape, F32, kind="ExternalInput").ap() for k, v in arrays.items()]
    out = nc.dram_tensor("out", (1, T, D), F32, kind="ExternalOutput").ap()
    mamba_and_experts(nc, *args, out)
    r = run(nc, [{f"in_{k}": v for k, v in arrays.items()}], core_ids=[0])
    return r.results[0]["out"]
```
